# Optimizing a Trainium2 kernel written in Bass

```python
import numpy as np
import jax
import jax.numpy as jnp

def _softmax(x, axis=-1):
    return jax.nn.softmax(x, axis=axis)
def _gelu(x):
    return jax.nn.gelu(x, approximate=True)
def _silu(x):
    return jax.nn.silu(x)
def _sigmoid(x):
    return jax.nn.sigmoid(x)
def _layernorm(x, axis=-1, eps=1e-5):
    m = jnp.mean(x, axis=axis, keepdims=True)
    v = jnp.var(x, axis=axis, keepdims=True)
    return (x - m) / jnp.sqrt(v + eps)
def _scatter_add(tgt, idx, src, axis=0):
    return tgt.at[idx].add(src)
def _segment_sum(src, seg, n):
    return jax.ops.segment_sum(src, seg, n)

kernel_name = 'mk_adj_resnorm_d4_adj_64_50afb9'

def setup_inputs(seed: int = 0):
    np.random.seed(seed)
    _w = jnp.asarray
    def _rec_inputs():
        import jax
        import jax.numpy as jnp
        _gk = jax.random.key(seed)
        x = -0.000929 + 1 * jax.random.normal(jax.random.fold_in(_gk, 1), (8, 2048, 64), jnp.float32)
        _a = jax.random.bernoulli(jax.random.fold_in(_gk, 2), 0.0078125, (8, 2048, 2048))
        _a = jnp.logical_or(_a, jnp.eye(2048, dtype=bool))
        adj = _a.astype(jnp.int32)
        return x, adj
    x, adj = _rec_inputs()
    def _L0_gnn_setup():
        import jax, jax.numpy as jnp
        import numpy as np
        B, N, F_IN, F_OUT = (8, 2048, 64, 64)
        ALPHA = 0.2
        NEG_INF = -9000000000000000.0
        LN_EPS = 1e-05
        key = jax.random.key(seed)
        ks = jax.random.split(key, 6)
        h = jax.random.normal(ks[0], (B, N, F_IN), dtype=jnp.float32)
        adj = jax.random.randint(ks[1], (B, N, N), 0, 2).astype(jnp.int32)
        adj = jnp.maximum(adj, jnp.eye(N, dtype=jnp.int32)[None])
        W = jax.random.normal(ks[2], (F_IN, F_OUT), dtype=jnp.float32) * 0.1
        a = jax.random.normal(ks[3], (2 * F_OUT,), dtype=jnp.float32) * 0.1
        W_res = jax.random.normal(ks[4], (F_IN, F_OUT), dtype=jnp.float32) * 0.1
        gamma = jnp.ones((F_OUT,), dtype=jnp.float32)
        beta = jnp.zeros((F_OUT,), dtype=jnp.float32)
        return {'h': h, 'adj': adj, 'W': W, 'a': a, 'W_res': W_res, 'gamma': gamma, 'beta': beta}
    _L0_gnn_all = _L0_gnn_setup()
    _L0_gnn_in = {k: v for k, v in _L0_gnn_all.items() if k in ('W', 'a', 'W_res', 'gamma', 'beta', )}
    del _L0_gnn_all

    def _L1_gnn_setup():
        import jax, jax.numpy as jnp
        import numpy as np
        NEG_BIG = -9000000000000000.0
        key = jax.random.key(seed)
        ks = jax.random.split(key, 6)
        B, N, C, F = (4, 4096, 64, 64)
        x = jax.random.normal(ks[0], (B, N, C), dtype=jnp.float32)
        adj = jax.random.randint(ks[1], (B, N, N), 0, 2, dtype=jnp.int32)
        W1 = jax.random.normal(ks[2], (C, F), dtype=jnp.float32) * (1.0 / np.sqrt(C))
        b1 = jnp.zeros((F,), dtype=jnp.float32)
        a1 = jax.random.normal(ks[3], (F,), dtype=jnp.float32) * (1.0 / np.sqrt(F))
        ba1 = jnp.zeros((1,), dtype=jnp.float32)
        a2 = jax.random.normal(ks[4], (F,), dtype=jnp.float32) * (1.0 / np.sqrt(F))
        ba2 = jnp.zeros((1,), dtype=jnp.float32)
        return {'x': x, 'adj': adj, 'W1': W1, 'b1': b1, 'a1': a1, 'ba1': ba1, 'a2': a2, 'ba2': ba2}
    _L1_gnn_all = _L1_gnn_setup()
    _L1_gnn_in = {k: v for k, v in _L1_gnn_all.items() if k in ('W1', 'b1', 'a1', 'ba1', 'a2', 'ba2', )}
    del _L1_gnn_all

    def _L2_gnn_setup():
        import jax, jax.numpy as jnp
        import numpy as np
        import math
        B, N, D, O, H = (2, 3072, 64, 64, 4)
        key = jax.random.key(seed)
        ks = jax.random.split(key, 8)
        x = jax.random.normal(ks[0], (B, N, D), dtype=jnp.float32)
        edge_index = jax.random.randint(ks[1], (B, N, N), 0, 2, dtype=jnp.int32)
        s = 1.0 / math.sqrt(D)
        Wv = jax.random.uniform(ks[2], (H, D, O), jnp.float32, -s, s)
        bv = jax.random.uniform(ks[3], (H, O), jnp.float32, -s, s)
        Wq = jax.random.uniform(ks[4], (H, D, O), jnp.float32, -s, s)
        bq = jax.random.uniform(ks[5], (H, O), jnp.float32, -s, s)
        Wk = jax.random.uniform(ks[6], (H, D, O), jnp.float32, -s, s)
        bk = jax.random.uniform(ks[7], (H, O), jnp.float32, -s, s)
        return {'x': x, 'edge_index': edge_index, 'Wv': Wv, 'bv': bv, 'Wq': Wq, 'bq': bq, 'Wk': Wk, 'bk': bk}
    _L2_gnn_all = _L2_gnn_setup()
    _L2_gnn_in = {k: v for k, v in _L2_gnn_all.items() if k in ('Wv', 'bv', 'Wq', 'bq', 'Wk', 'bk', )}
    del _L2_gnn_all

    def _L3_gnn_setup():
        import jax, jax.numpy as jnp
        import numpy as np
        B, N, D = (4, 4096, 64)
        key = jax.random.key(seed)
        k1, k2, k3 = jax.random.split(key, 3)
        x = jax.random.normal(k1, (B, N, D), dtype=jnp.float32)
        adj = jax.random.randint(k2, (B, N, N), 0, 2, dtype=jnp.int32)
        beta = jax.random.uniform(k3, (1,), dtype=jnp.float32)
        bias = jnp.array([1e-07], dtype=jnp.float32)
        return {'x': x, 'adj': adj, 'beta': beta, 'bias': bias}
    _L3_gnn_all = _L3_gnn_setup()
    _L3_gnn_in = {k: v for k, v in _L3_gnn_all.items() if k in ('beta', 'bias', )}
    del _L3_gnn_all

    return {
        "x": x,
        "adj": adj,
        "L0_gnn_W": _L0_gnn_in["W"],
        "L0_gnn_a": _L0_gnn_in["a"],
        "L0_gnn_W_res": _L0_gnn_in["W_res"],
        "L0_gnn_gamma": _L0_gnn_in["gamma"],
        "L0_gnn_beta": _L0_gnn_in["beta"],
        "L1_gnn_W1": _L1_gnn_in["W1"],
        "L1_gnn_b1": _L1_gnn_in["b1"],
        "L1_gnn_a1": _L1_gnn_in["a1"],
        "L1_gnn_ba1": _L1_gnn_in["ba1"],
        "L1_gnn_a2": _L1_gnn_in["a2"],
        "L1_gnn_ba2": _L1_gnn_in["ba2"],
        "L2_gnn_Wv": _L2_gnn_in["Wv"],
        "L2_gnn_bv": _L2_gnn_in["bv"],
        "L2_gnn_Wq": _L2_gnn_in["Wq"],
        "L2_gnn_bq": _L2_gnn_in["bq"],
        "L2_gnn_Wk": _L2_gnn_in["Wk"],
        "L2_gnn_bk": _L2_gnn_in["bk"],
        "L3_gnn_beta": _L3_gnn_in["beta"],
        "L3_gnn_bias": _L3_gnn_in["bias"],
    }

def reference(x, adj, L0_gnn_W, L0_gnn_a, L0_gnn_W_res, L0_gnn_gamma, L0_gnn_beta, L1_gnn_W1, L1_gnn_b1, L1_gnn_a1, L1_gnn_ba1, L1_gnn_a2, L1_gnn_ba2, L2_gnn_Wv, L2_gnn_bv, L2_gnn_Wq, L2_gnn_bq, L2_gnn_Wk, L2_gnn_bk, L3_gnn_beta, L3_gnn_bias):
    import jax
    import jax.numpy as jnp
    def _L0_gnn_ref(h, adj, W, a, W_res, gamma, beta):
        import jax, jax.numpy as jnp
        import numpy as np
        B, N, F_IN, F_OUT = (8, 2048, 64, 64)
        ALPHA = 0.2
        NEG_INF = -9000000000000000.0
        LN_EPS = 1e-05
        Wh = h @ W
        src = Wh @ a[:F_OUT]
        dst = Wh @ a[F_OUT:]
        e = jax.nn.leaky_relu(src[:, :, None] + dst[:, None, :], ALPHA)
        e = jnp.where(adj > 0, e, NEG_INF)
        attention = jax.nn.softmax(e, axis=-1)
        h_prime = jnp.einsum('bij,bjf->bif', attention, Wh)
        h_prime = h_prime + h @ W_res
        h_prime = jax.nn.elu(h_prime)
        mean = jnp.mean(h_prime, axis=-1, keepdims=True)
        var = jnp.var(h_prime, axis=-1, keepdims=True)
        return (h_prime - mean) * jax.lax.rsqrt(var + LN_EPS) * gamma + beta

    def _L1_gnn_ref(x, adj, W1, b1, a1, ba1, a2, ba2):
        import jax, jax.numpy as jnp
        import numpy as np
        NEG_BIG = -9000000000000000.0
        seq_fts = jnp.einsum('bnc,cf->bnf', x, W1) + b1
        f1 = seq_fts @ a1 + ba1[0]
        f2 = seq_fts @ a2 + ba2[0]
        logits = f1[:, None, :] + f2[:, :, None]
        logits = jax.nn.leaky_relu(logits, negative_slope=0.01)
        attention = jnp.where(adj > 0, logits, jnp.float32(NEG_BIG))
        coefs = jax.nn.softmax(attention, axis=1)
        ret = jnp.einsum('bij,bjf->bif', coefs, seq_fts)
        return jax.nn.elu(ret)

    def _L2_gnn_ref(x, edge_index, Wv, bv, Wq, bq, Wk, bk):
        import jax, jax.numpy as jnp
        import numpy as np
        import math
        B, N, D, O, H = (2, 3072, 64, 64, 4)
        dk = jnp.asarray(math.sqrt(x.shape[-1]), x.dtype)
        v = jnp.einsum('bnd,hdo->bhno', x, Wv) + bv[None, :, None, :]
        q = jnp.einsum('bnd,hdo->bhno', x, Wq) + bq[None, :, None, :]
        k = jnp.einsum('bnd,hdo->bhno', x, Wk) + bk[None, :, None, :]
        scores = jnp.einsum('bhno,bhmo->bhnm', q, k) / dk
        scores = jax.nn.leaky_relu(scores, 0.2)
        mask = -10000000000.0 * (1.0 - edge_index.astype(scores.dtype))
        scores = scores + mask[:, None, :, :]
        prop = jax.nn.softmax(scores, axis=-1)
        feats = jnp.einsum('bhnm,bhmo->bhno', prop, v)
        out = jnp.mean(feats, axis=1)
        return jax.nn.leaky_relu(out, 0.2)

    def _L3_gnn_ref(x, adj, beta, bias):
        import jax, jax.numpy as jnp
        import numpy as np
        B, N, D = (4, 4096, 64)
        norm2 = jnp.linalg.norm(x, ord=2, axis=2, keepdims=True)
        dots = jnp.einsum('bnd,bmd->bnm', x, x)
        denom = jnp.einsum('bni,bmi->bnm', norm2, norm2) + bias
        cos = beta * (dots / denom)
        mask = (1.0 - adj.astype(x.dtype)) * -1000000000.0
        P = jax.nn.softmax(cos + mask, axis=1)
        return jnp.einsum('bnm,bmd->bnd', P, x)

    x = _layernorm(x + _L0_gnn_ref(x, adj, L0_gnn_W, L0_gnn_a, L0_gnn_W_res, L0_gnn_gamma, L0_gnn_beta), axis=-1)
    x = _layernorm(x + _L1_gnn_ref(x, adj, L1_gnn_W1, L1_gnn_b1, L1_gnn_a1, L1_gnn_ba1, L1_gnn_a2, L1_gnn_ba2), axis=-1)
    x = _layernorm(x + _L2_gnn_ref(x, adj, L2_gnn_Wv, L2_gnn_bv, L2_gnn_Wq, L2_gnn_bq, L2_gnn_Wk, L2_gnn_bk), axis=-1)
    x = _layernorm(x + _L3_gnn_ref(x, adj, L3_gnn_beta, L3_gnn_bias), axis=-1)
    return x


_drawn_inputs = setup_inputs


def setup_inputs(seed=0):
    import zlib

    import numpy as np

    out = dict(_drawn_inputs(seed))
    spreads = {'L0_gnn_gamma': (1.0, 0.2), 'L0_gnn_beta': (0.0, 0.1), 'L1_gnn_b1': (0.0, 0.1)}
    factors = {'L2_gnn_Wq': 4.607, 'L2_gnn_bq': 8.0, 'L2_gnn_Wk': 4.546, 'L2_gnn_bk': 64.0}
    for name, (base, spread) in spreads.items():
        noise = np.random.default_rng([zlib.crc32(name.encode()), seed]).standard_normal(out[name].shape)
        drawn = base * np.exp(spread * noise) if base else spread * noise
        out[name] = jnp.asarray(drawn.astype(out[name].dtype))
    for name, factor in factors.items():
        out[name] = (out[name] * factor).astype(out[name].dtype)
    return out
```

```python
from contextlib import ExitStack

import concourse.bass as bass
from concourse import mybir

F32 = mybir.dt.float32
BF16 = mybir.dt.bfloat16
I32 = mybir.dt.int32
ALU = mybir.AluOpType
ACT = mybir.ActivationFunctionType
AX = mybir.AxisListType.X

P = 128
BANK = 512
NO_EDGE = 9.0e15
LOWEST = -3.0e38
GAT_SLOPE = 0.2
COL_SLOPE = 0.01
EPS = 1e-5
HEADS = 4


def build(nc, x, adj, w0, w0_t, a0, gamma, beta, w1, w1_t, b1, a1, ba1, a2, ba2,
          wv, bv, wq, bq, wk, bk, cos_beta, cos_bias, out):
    B, N, D = x.shape
    T = N // P
    GROUP = BANK // P
    G = T // GROUP
    HALF = N // 2
    C = HEADS * D
    assert D * 2 == P and T == GROUP * G and N == 4 * BANK

    ctx = ExitStack()
    with ctx:
        def sb(name, shape, dt=F32):
            return ctx.enter_context(nc.sbuf_tensor(name, shape, dt))

        def sem(name):
            return ctx.enter_context(nc.semaphore(name))

        mask = sb("mask", [P, T, N], BF16)
        turned = sb("turned", [P, T, BANK])
        probs = sb("probs", [P, 2, N])
        relus = sb("relus", [P, 2, HALF])
        feat_t = sb("feat_t", [P, N])
        q_hh = sb("q_hh", [P, N], BF16)
        q_mm = sb("q_mm", [P, N], BF16)
        q_hl = sb("q_hl", [P, N], BF16)
        k_hm = sb("k_hm", [P, N], BF16)
        k_lh = sb("k_lh", [P, N], BF16)
        values = sb("values", [P, T, C])
        v_head = sb("v_head", [P, T, D])
        nodes = sb("nodes", [P, T, D])
        mixed = sb("mixed", [P, T, D])
        tmp_a = sb("tmp_a", [P, T, D])
        tmp_b = sb("tmp_b", [P, T, D])
        denom = sb("denom", [P, T])
        inv = sb("inv", [P, T])
        rowmax = sb("rowmax", [P, 2, 2])
        shift = sb("shift", [P, 2])
        folded_in = sb("folded_in", [P, BANK])
        stat_a = sb("stat_a", [P, T])
        stat_b = sb("stat_b", [P, T])
        norms = sb("norms", [P, T])
        ident = sb("ident", [P, P])
        ident_b = sb("ident_b", [P, P], BF16)
        fold = sb("fold", [P, D])
        ones = sb("ones", [P, P])
        minus_half = sb("minus_half", [P, T])
        plus_half = sb("plus_half", [P, T])
        w0_sb = sb("w0_sb", [P, 2 * D])
        w1_sb = sb("w1_sb", [P, D])
        wv_sb = sb("wv_sb", [P, C])
        wq_sb = sb("wq_sb", [P, HEADS, P])
        wk_sb = sb("wk_sb", [P, HEADS, P])
        wq_h = sb("wq_h", [P, P])
        wk_h = sb("wk_h", [P, P])
        w0t_sb = sb("w0t_sb", [D, D])
        w1t_sb = sb("w1t_sb", [D, D])
        line_w = sb("line_w", [P, 4, P])
        a_cols = sb("a_cols", [D, 4])
        a_wide = sb("a_wide", [D, 4, P])
        b1_col = sb("b1_col", [D, 1])
        b1_wide = sb("b1_wide", [D, P])
        ba_cols = sb("ba_cols", [P, 2])
        line_bias = sb("line_bias", [P, 4])
        b1_row = sb("b1_row", [P, D])
        bv_row = sb("bv_row", [P, C])
        gamma_row = sb("gamma_row", [P, D])
        beta_row = sb("beta_row", [P, D])
        bq_col = sb("bq_col", [P, HEADS])
        bk_col = sb("bk_col", [P, HEADS])
        cos_cols = sb("cos_cols", [P, 2])
        picks = sb("picks", [P, 8])
        adj_in = turned[:, :, :].rearrange("p a b -> p (a b)").rearrange(
            "p (s n) -> p s n", s=GROUP).bitcast(I32)
        probs_t = turned[:, :, :].rearrange("p a b -> p (a b)").rearrange("p (s n) -> p s n", s=GROUP)
        lines = probs
        twice = probs[:, 0, :].rearrange("p (t e) -> p t e", t=T)
        halves = probs[:, 0, :]
        norm_row = probs[:, 1, :]
        v_norm = folded_in[:, 0:GROUP * D].rearrange("p (s d) -> p s d", s=GROUP)
        part_a = q_mm
        part_b = q_hl
        spare = relus[:, :, :].rearrange("p a b -> p (a b)")

        ps = ctx.enter_context(nc.psum_tensor("ps", [P, 8 * BANK], F32))
        S0, T0, O0, M0 = 0, N, N + 2 * BANK, N + 3 * BANK

        r_scores = sem("r_scores")
        r_relu = sem("r_relu")
        r_scaled = sem("r_scaled")
        r_shift = sem("r_shift")
        r_probs = sem("r_probs")
        r_turned = sem("r_turned")
        r_evac_dve = sem("r_evac_dve")
        r_evac_act = sem("r_evac_act")
        r_product = sem("r_product")
        r_prod_out = sem("r_prod_out")
        r_folded = sem("r_folded")
        r_inv = sem("r_inv")
        r_mixed = sem("r_mixed")
        r_lrn = sem("r_lrn")

        start_at_one = (r_evac_act, r_evac_dve, r_product, r_prod_out, r_folded, r_mixed)

        landed = sem("landed")
        zeroed = sem("zeroed")
        made = sem("made")
        loads = [
            (w0_sb[0:D, 0:2 * D], w0), (w1_sb[0:D, :], w1), (wv_sb[0:D, :], wv),
            (wq_sb[0:D, :, 0:D], wq), (wq_sb[0:D, :, D:P], wq),
            (wk_sb[0:D, :, 0:D], wk), (wk_sb[0:D, :, D:P], wk),
            (w0t_sb[:, :], w0_t), (w1t_sb[:, :], w1_t),
            (a_cols[:, 0:2], a0), (a_cols[:, 2:3], a1), (a_cols[:, 3:4], a2), (b1_col[:, :], b1.rearrange("a d -> d a")),
            (ba_cols[:, 0:1], ba1.to_broadcast([P, 1])), (ba_cols[:, 1:2], ba2.to_broadcast([P, 1])),
            (b1_row[:, :], b1.to_broadcast([P, D])), (bv_row[:, :], bv.to_broadcast([P, C])),
            (gamma_row[:, :], gamma.to_broadcast([P, D])), (beta_row[:, :], beta.to_broadcast([P, D])),
            (bq_col[0:D, :], bq), (bq_col[D:P, :], bq), (bk_col[0:D, :], bk), (bk_col[D:P, :], bk),
            (cos_cols[:, 0:1], cos_beta.to_broadcast([P, 1])), (cos_cols[:, 1:2], cos_bias.to_broadcast([P, 1])),
        ]
        with nc.Block() as block:
            @block.sync
            def _(sp):
                sp.wait_ge(zeroed, 8)
                for dst, src in loads:
                    sp.dma_start(dst, src).then_inc(landed, 16)

            @block.gpsimd
            def _(pool):
                for t in (w0_sb, w1_sb, wv_sb, wq_sb, wk_sb, line_w, ident, line_bias):
                    pool.memset(t[:], 0.0).then_inc(zeroed, 1)
                for n, freed in enumerate(start_at_one):
                    part = slice(n * P // len(start_at_one), (n + 1) * P // len(start_at_one))
                    pool.memset(ones[:, part], 1.0).then_inc(freed, 1)
                pool.memset(plus_half[:], 0.5)
                pool.memset(minus_half[:], -0.5)
                pool.wait_ge(zeroed, 8)
                pool.affine_select(out=ident[:], in_=ident[:], compare_op=ALU.not_equal, fill=1.0, base=0,
                                   pattern=[[-1, P]], channel_multiplier=1).then_inc(made, 1)

            @block.vector
            def _(dve):
                dve.wait_ge(made, 1)
                dve.tensor_copy(ident_b[:], ident[:]).then_inc(made, 1)
                dve.tensor_tensor(fold[:], ident[:, 0:D], ident[:, D:P], ALU.add).then_inc(made, 1)
                for c, (lo, hi) in enumerate(((1, 3), (2, 3), (0, 3), (3, 6), (4, 6), (5, 6))):
                    sign = c not in (2, 3)
                    dve.tensor_reduce(picks[:, c:c + 1], ident[:, lo:hi], AX, ALU.add, negate=sign).then_inc(made, 1)
                dve.wait_ge(landed, 16 * len(loads))
                dve.tensor_copy(a_wide[:], a_cols[:, :].unsqueeze(2).to_broadcast([D, 4, P])).then_inc(made, 1)
                dve.tensor_copy(b1_wide[:], b1_col[:].to_broadcast([D, P])).then_inc(made, 1)
                dve.tensor_scalar(bq_col[:], bq_col[:], float(D) ** -0.5, None, ALU.mult).then_inc(made, 1)

            @block.tensor
            def _(pe):
                pe.wait_ge(made, 12)
                pe.wait_ge(landed, 16 * len(loads))
                for c, wt in enumerate((w0t_sb, w0t_sb, w1t_sb, w1t_sb)):
                    pe.matmul(ps[0:D, c * P:(c + 1) * P], wt[:], a_wide[:, c, :], start=True, stop=True).then_inc(made, 1)
                for c in range(2):
                    pe.matmul(ps[:, BANK + c:BANK + c + 1], b1_wide[:], a_cols[:, 2 + c:3 + c],
                              start=True, stop=True).then_inc(made, 1)

            @block.scalar
            def _(act):
                act.preload_act_table_set("natural_log_exp_and_others")
                act.wait_ge(made, 18)
                act.activation(line_w[0:D, :, :], ps[0:D, 0:4 * P].rearrange("p (a b) -> p a b", a=4), ACT.Copy)
                for c in range(2):
                    act.activation(line_bias[:, 2 + c:3 + c], ps[:, BANK + c:BANK + c + 1], ACT.Identity,
                                   bias=ba_cols[:, c:c + 1])

        bounds = {}

        def wait_apart(eng, semaphore, value):
            if eng.engine not in bounds:
                bounds[eng.engine] = eng.alloc_register(f"bound_{len(bounds)}")
            bound = bounds[eng.engine]
            eng.reg_mov(bound, value)
            eng.wait_ge(made, 1)
            eng.wait_ge(semaphore, bound)

        x_landed = sem("x_landed")
        adj_landed = [sem(f"adj_landed{s}") for s in range(GROUP)]
        adj_used = sem("adj_used")

        def load(b):
            with nc.Block() as block:
                @block.sync
                def _(sp):
                    sp.dma_start(nodes[:], x[b].rearrange("(t p) d -> p t d", p=P)).then_inc(x_landed, 16)
                    rows = adj.rearrange("b (t p) j -> b t p j", p=P)

                    def group(g, first):
                        for s in range(GROUP):
                            if not first:
                                sp.wait_ge(adj_used, b * T + g * GROUP + (s + 1 - GROUP))
                            sp.dma_start(adj_in[:, s, :], rows[b, g * GROUP + s]).then_inc(adj_landed[s], 16)
                    group(0, True)
                    with sp.Fori(1, G) as g:
                        group(g, False)

                @block.vector
                def _(dve):
                    with dve.Fori(0, G) as g:
                        for s in range(GROUP):
                            dve.wait_ge(adj_landed[s], b * (16 * G) + g * 16 + 16)
                            dve.tensor_scalar(mask[:, g * GROUP + s, :], adj_in[:, s, :], 1.0, NO_EDGE,
                                              ALU.subtract, ALU.mult).then_inc(adj_used, 1)
                    wait_apart(dve, x_landed, b * 16 + 16)

        doubled = sem("doubled")
        xt_ready = sem("xt_ready")
        xt_copied = sem("xt_copied")

        def transpose_nodes(turn):
            with nc.Block() as block:
                @block.gpsimd
                def _(pool):
                    pool.tensor_scalar(twice[:, :, D:P], nodes[:], 1.0, 0.0, ALU.mult, ALU.add).then_inc(doubled, 1)

                @block.vector
                def _(dve):
                    dve.tensor_copy(twice[:, :, 0:D], nodes[:]).then_inc(doubled, 1)
                    for q in (1, 3):
                        dve.wait_ge(xt_ready, turn * 4 + q + 1)
                        dve.tensor_copy(feat_t[:, q * BANK:(q + 1) * BANK], ps[:, q * BANK:(q + 1) * BANK])

                @block.tensor
                def _(pe):
                    pe.wait_ge(doubled, turn * 2 + 2)
                    for t in range(T):
                        mm = pe.transpose(ps[:, t * P:(t + 1) * P], twice[:, t, :], ident[:])
                        if t % 4 == 3:
                            mm.then_inc(xt_ready, 1)

                @block.scalar
                def _(act):
                    for q in (0, 2):
                        act.wait_ge(xt_ready, turn * 4 + q + 1)
                        act.activation(feat_t[:, q * BANK:(q + 1) * BANK], ps[:, q * BANK:(q + 1) * BANK], ACT.Copy)

        line_ready = sem("line_ready")
        line_copied = sem("line_copied")
        line_split = sem("line_split")

        def line_operands(turn, which):
            with nc.Block() as block:
                @block.tensor
                def _(pe):
                    for r in range(2):
                        for q in range(4):
                            c = r * N + q * BANK
                            mm = pe.matmul(ps[:, c:c + BANK], line_w[:, which + r, :],
                                           feat_t[:, q * BANK:(q + 1) * BANK], start=True, stop=True)
                        mm.then_inc(line_ready, 1)

                @block.scalar
                def _(act):
                    for r in range(2):
                        act.wait_ge(line_ready, turn * 2 + r + 1)
                        act.activation(lines[:, r, :], ps[:, r * N:(r + 1) * N], ACT.Identity,
                                       bias=line_bias[:, which + r:which + r + 1]).then_inc(line_copied, 1)

                @block.vector
                def _(dve):
                    step = turn * 10
                    for r, operand in enumerate((q_hh, k_hm)):
                        line = lines[:, r, :]
                        late, last, own, other = ((0, 1, 2, 3), (4, 5, 3, 2))[r]
                        dve.wait_ge(line_copied, turn * 2 + r + 1)
                        for c in (late, last):
                            dve.tensor_copy(part_a[:], line).then_inc(line_split, 1)
                            step = step + 1
                            dve.wait_ge(line_split, step)
                            dve.scalar_tensor_tensor(line, part_a[:], picks[:, c:c + 1], line,
                                                     ALU.mult, ALU.add).then_inc(line_split, 1)
                            step = step + 1
                            dve.wait_ge(line_split, step)
                        dve.tensor_scalar(operand[:], line, picks[:, own:own + 1], picks[:, other:other + 1],
                                          ALU.mult, ALU.add).then_inc(line_split, 1)
                        step = step + 1

        v_ready = sem("v_ready")

        def node_values(turn, width, weights, bias_row):
            with nc.Block() as block:
                @block.tensor
                def _(pe):
                    for t in range(T):
                        mm = pe.matmul(ps[:, t * width:(t + 1) * width], feat_t[:, t * P:(t + 1) * P],
                                       weights[:, 0:width], start=True, stop=True)
                        if t % 4 == 3:
                            mm.then_inc(v_ready, 1)

                @block.vector
                def _(dve):
                    for q in range(4):
                        dve.wait_ge(v_ready, turn * 4 + (q + 1 if width > D else q // 2 * 2 + 2))
                        src = ps[:, q * 4 * width:(q + 1) * 4 * width].rearrange("p (t c) -> p t c", t=4)
                        dst = values[:, q * 4:(q + 1) * 4, 0:width]
                        if bias_row is None:
                            dve.tensor_copy(dst, src)
                        else:
                            dve.tensor_tensor(dst, src, bias_row[:].unsqueeze(1).to_broadcast([P, 4, width]), ALU.add)

        picked = sem("picked")
        qk_ready = sem("qk_ready")
        qk_copied = sem("qk_copied")
        qk_split = sem("qk_split")

        def split_q_k(dve, base, copied_base, q, k):
            lo, up = slice(0, D), slice(D, P)
            dve.wait_ge(qk_copied, copied_base + 1)
            dve.tensor_copy(q_hh[:], q).then_inc(qk_split, 1)
            dve.wait_ge(qk_split, base + 1)
            dve.tensor_tensor(q, q, q_hh[:], ALU.subtract).then_inc(qk_split, 1)
            dve.tensor_copy(q_hl[lo, :], q_hh[lo, :])
            dve.wait_ge(qk_split, base + 2)
            dve.tensor_copy(q_mm[:], q).then_inc(qk_split, 1)
            dve.wait_ge(qk_split, base + 3)
            dve.tensor_tensor(q_hl[up, :], q[up, :], q_mm[up, :], ALU.subtract)
            dve.wait_ge(qk_copied, copied_base + 2)
            dve.tensor_copy(k_hm[:], k).then_inc(qk_split, 1)
            dve.wait_ge(qk_split, base + 4)
            dve.tensor_copy(k_lh[up, :], k_hm[up, :]).then_inc(qk_split, 1)
            dve.tensor_tensor(k, k, k_hm[:], ALU.subtract).then_inc(qk_split, 1)
            dve.wait_ge(qk_split, base + 6)
            dve.tensor_copy(k_hm[up, :], k[up, :])
            dve.tensor_copy(k_lh[lo, :], k[lo, :]).then_inc(qk_split, 1)
            dve.wait_ge(qk_split, base + 7)
            dve.tensor_tensor(k_lh[lo, :], k[lo, :], k_lh[lo, :], ALU.subtract).then_inc(qk_split, 1)

        def head_operands(b, h):
            turn = b * HEADS + h
            with nc.Block() as block:
                @block.scalar
                def _(act):
                    act.activation(wq_h[:], wq_sb[:, h, :], ACT.Copy).then_inc(picked, 1)
                    act.activation(wk_h[:], wk_sb[:, h, :], ACT.Copy).then_inc(picked, 1)
                    act.activation(v_head[:], values[:, :, bass.ds(h * D, D)], ACT.Copy)
                    wait_apart(act, qk_ready, turn * 2 + 1)
                    act.activation(lines[:, 0, :], ps[:, 0:N], ACT.Identity, bias=bq_col[:, bass.ds(h, 1)],
                                   scale=float(D) ** -0.5).then_inc(qk_copied, 1)
                    wait_apart(act, qk_ready, turn * 2 + 2)
                    act.activation(lines[:, 1, :], ps[:, N:2 * N], ACT.Identity,
                                   bias=bk_col[:, bass.ds(h, 1)]).then_inc(qk_copied, 1)

                @block.tensor
                def _(pe):
                    for r, w in enumerate((wq_h, wk_h)):
                        pe.wait_ge(picked, turn * 2 + r + 1)
                        for q in range(4):
                            c = r * N + q * BANK
                            mm = pe.matmul(ps[:, c:c + BANK], w[:], feat_t[:, q * BANK:(q + 1) * BANK],
                                           start=True, stop=True)
                        mm.then_inc(qk_ready, 1)

                @block.vector
                def _(dve):
                    split_q_k(dve, (turn + b) * 8, (turn + b) * 2, lines[:, 0, :], lines[:, 1, :])

        def attention_rows(turn, passes, average):
            n0 = turn * T
            g0 = turn * G

            def groups(eng, body):
                body(0, True, False)
                with eng.Fori(1, G - 1) as g:
                    body(g, False, False)
                body(G - 1, False, True)

            with nc.Block() as block:
                @block.tensor
                def _(pe):
                    def scores(g, k, first):
                        tile = g * GROUP + k
                        for hf in range(2):
                            if not first:
                                pe.wait_ge(r_scaled, n0 * 2 + g * (2 * GROUP) + (2 * k + hf - 1))
                            for q in range(2):
                                col = hf * HALF + q * BANK
                                dst = ps[:, S0 + col:S0 + col + BANK]
                                for n, (a, c) in enumerate(passes):
                                    pe.matmul(dst, a[:, bass.ds(tile * P, P)], c[:, col:col + BANK],
                                              start=(n == 0), stop=False)
                                mm = pe.matmul(dst, ident_b[:], mask[:, tile, col:col + BANK],
                                               start=False, stop=True)
                            mm.then_inc(r_scores, 1)

                    def transposes(g, k):
                        pe.wait_ge(r_probs, n0 + g * GROUP + (k + 1))
                        for c in range(4):
                            seen = n0 * 2 + g * (2 * GROUP) + (2 * k + (c >= 2) + 1)
                            pe.wait_ge((r_evac_act, r_evac_dve, r_evac_dve, r_evac_act)[c], seen)
                            bank = T0 + (c % 2) * BANK
                            for u in range(4):
                                j = 4 * c + u
                                mm = pe.transpose(ps[:, bank + u * P:bank + (u + 1) * P],
                                                  probs[:, k % 2, j * P:(j + 1) * P], ident[:])
                            mm.then_inc(r_turned, 1)

                    def product(g):
                        pe.wait_ge(r_evac_act, n0 * 2 + g * (2 * GROUP) + (2 * GROUP + 1))
                        pe.wait_ge(r_evac_dve, n0 * 2 + g * (2 * GROUP) + (2 * GROUP + 1))
                        pe.wait_ge(r_prod_out, g0 + g + 1)
                        for j in range(T):
                            half = (j % 2) * D
                            mm = pe.matmul(ps[half:half + D, O0:O0 + BANK], v_head[:, j, :], turned[:, j, :],
                                           start=(j < 2), stop=(j >= T - 2))
                        mm.then_inc(r_product, 1)

                    def fold_product(g):
                        pe.wait_ge(r_prod_out, g0 + g + 2)
                        pe.wait_ge(r_mixed, g0 + g + 1)
                        for k in range(GROUP):
                            mm = pe.matmul(ps[:, M0 + k * D:M0 + (k + 1) * D], folded_in[:, k * P:(k + 1) * P],
                                           fold[:], start=True, stop=True)
                        mm.then_inc(r_folded, 1)

                    def body(g, first, last):
                        for k in range(GROUP):
                            if not (last and k == GROUP - 1):
                                scores(g, k + 1, False)
                            if k == 0 and not first:
                                product(g - 1)
                            transposes(g, k)
                            if k == 0 and not first:
                                fold_product(g - 1)

                    scores(0, 0, True)
                    groups(pe, body)
                    product(G - 1)
                    fold_product(G - 1)

                @block.scalar
                def _(act):
                    def evacuate(g, k, slot):
                        for c in (1, 2):
                            act.wait_ge(r_turned, n0 * 4 + g * (4 * GROUP) + (4 * k + c + 1))
                            if k == 0:
                                act.wait_ge(r_product, g0 + g + 1)
                            bank = T0 + (c % 2) * BANK
                            act.activation(turned[:, 4 * c:4 * c + 4, k * P:(k + 1) * P],
                                           ps[:, bank:bank + BANK].rearrange("p (a b) -> p a b", a=4),
                                           ACT.Copy).then_inc(r_evac_act, 1)

                    def copy_product(g):
                        act.wait_ge(r_product, g0 + g + 2)
                        act.wait_ge(r_folded, g0 + g + 1)
                        act.activation(folded_in[:], ps[:, O0:O0 + BANK], ACT.Copy).then_inc(r_prod_out, 1)

                    def body(g, first, last):
                        for k in range(GROUP):
                            for hf in range(2):
                                act.wait_ge(r_scores, n0 * 2 + g * (2 * GROUP) + (2 * k + hf + 1))
                                act.activation(relus[:, hf, :], ps[:, S0 + hf * HALF:S0 + (hf + 1) * HALF],
                                               ACT.Relu, scale=1.0 / GAT_SLOPE - 1.0).then_inc(r_relu, 1)
                            if k == 1 and not first:
                                copy_product(g - 1)
                            if k >= 1:
                                evacuate(g, k - 1, k)
                            elif not first:
                                evacuate(g - 1, GROUP - 1, k)
                            wait_apart(act, r_shift, n0 + g * GROUP + (k + 1))
                            act.activation(probs[:, k % 2, :], probs[:, k % 2, :], ACT.Exp,
                                           bias=shift[:, k % 2:k % 2 + 1],
                                           accum_out=denom[:, bass.ds(g * GROUP + k, 1)]).then_inc(r_probs, 1)

                    groups(act, body)
                    evacuate(G - 1, GROUP - 1, 0)
                    copy_product(G - 1)

                @block.vector
                def _(dve):
                    def leaky(g, k, hf, first):
                        if hf == 0 and not (first and k < 2):
                            dve.wait_ge(r_turned, n0 * 4 + g * (4 * GROUP) + (4 * k - 4))
                        wait_apart(dve, r_relu, n0 * 2 + g * (2 * GROUP) + (2 * k + hf + 1))
                        dve.tensor_tensor_reduce(
                            probs[:, k % 2, hf * HALF:(hf + 1) * HALF], ps[:, S0 + hf * HALF:S0 + (hf + 1) * HALF],
                            relus[:, hf, :], GAT_SLOPE, LOWEST, ALU.add, ALU.max,
                            rowmax[:, k % 2, hf:hf + 1]).then_inc(r_scaled, 1)

                    def evacuate(g, k, c):
                        dve.wait_ge(r_turned, n0 * 4 + g * (4 * GROUP) + (4 * k + c + 1))
                        if k == 0 and c == 0:
                            dve.wait_ge(r_product, g0 + g + 1)
                        bank = T0 + (c % 2) * BANK
                        dve.tensor_copy(turned[:, 4 * c:4 * c + 4, k * P:(k + 1) * P],
                                        ps[:, bank:bank + BANK].rearrange("p (a b) -> p a b", a=4)).then_inc(r_evac_dve, 1)

                    def mix(g):
                        dve.wait_ge(r_probs, n0 + g * GROUP + GROUP)
                        zs = inv[:, bass.ds(g * GROUP, GROUP)]
                        dve.reciprocal(zs, denom[:, bass.ds(g * GROUP, GROUP)]).then_inc(r_inv, 1)
                        dve.wait_ge(r_folded, g0 + g + 2)
                        dve.wait_ge(r_inv, g0 + g + 1)
                        prod = ps[:, M0:M0 + GROUP * D].rearrange("p (a b) -> p a b", a=GROUP)
                        scale = zs.unsqueeze(2).to_broadcast([P, GROUP, D])
                        dst = mixed[:, bass.ds(g * GROUP, GROUP), :]
                        if average:
                            part = tmp_a[:, 0:GROUP, :]
                            dve.tensor_tensor(part, prod, scale, ALU.mult).then_inc(r_mixed, 1)
                            dve.wait_ge(r_mixed, g0 + g + 2)
                            dve.scalar_tensor_tensor(dst, part, 1.0 / HEADS, dst, ALU.mult, ALU.add)
                        else:
                            dve.tensor_tensor(dst, prod, scale, ALU.mult).then_inc(r_mixed, 1)

                    def body(g, first, last):
                        for k in range(GROUP):
                            leaky(g, k, 0, first)
                            before = (g, k - 1) if k >= 1 else (g - 1, GROUP - 1)
                            skip = first and k == 0
                            if not skip:
                                evacuate(*before, 0)
                            leaky(g, k, 1, first)
                            dve.wait_ge(r_scaled, n0 * 2 + g * (2 * GROUP) + (2 * k + 2))
                            dve.tensor_reduce(shift[:, k % 2:k % 2 + 1], rowmax[:, k % 2, :], AX, ALU.max,
                                              negate=True).then_inc(r_shift, 1)
                            if not skip:
                                evacuate(*before, 3)
                            if k == 1 and not first:
                                mix(g - 1)

                    groups(dve, body)
                    evacuate(G - 1, GROUP - 1, 0)
                    evacuate(G - 1, GROUP - 1, 3)
                    mix(G - 1)

        c_scores = sem("c_scores")
        c_relu = sem("c_relu")
        c_cos = sem("c_cos")
        c_scaled = sem("c_scaled")
        c_shift = sem("c_shift")
        c_probs = sem("c_probs")
        c_inv = sem("c_inv")
        c_values = sem("c_values")
        c_product = sem("c_product")
        c_prod_out = sem("c_prod_out")
        c_folded = sem("c_folded")

        def attention_columns(b, cosine):
            turn = b * 2 + (1 if cosine else 0)
            n0 = turn * T
            p0 = turn * (T // 2)
            m0 = b * (2 * T)

            def groups(eng, body):
                body(0, True)
                with eng.Fori(1, G) as g:
                    body(g, False)

            with nc.Block() as block:
                @block.tensor
                def _(pe):
                    def edges(dst, tile, i0, first_in_bank):
                        for u in range(4):
                            mm = pe.matmul(dst[:, u * P:(u + 1) * P], mask[:, i0 + u, bass.ds(tile * P, P)],
                                           ident_b[:], start=(first_in_bank and u == 0),
                                           stop=(u == 3), skip_group_check=True)
                        return mm

                    def scores(g, k, first):
                        tile = g * GROUP + k
                        for hf in range(2):
                            half = 2 * k + hf
                            if cosine:
                                if not (first and half == 0):
                                    pe.wait_ge(c_scaled, n0 * 2 + g * (2 * GROUP) + half)
                            elif not (first and half < 2):
                                pe.wait_ge(c_scaled, n0 * 2 + g * (2 * GROUP) + (half - 1))
                            for q in range(2):
                                col = hf * HALF + q * BANK
                                if cosine:
                                    dst = ps[:, S0 + q * BANK:S0 + (q + 1) * BANK]
                                    for n, (a, c) in enumerate(((q_hh, k_hm), (q_mm, k_hm), (q_hl, k_lh))):
                                        pe.matmul(dst, a[:, bass.ds(tile * P, P)], c[:, col:col + BANK],
                                                  start=(n == 0), stop=(n == 2))
                                    mm = edges(ps[:, S0 + HALF + q * BANK:S0 + HALF + (q + 1) * BANK],
                                               tile, col // P, True)
                                else:
                                    dst = ps[:, S0 + col:S0 + col + BANK]
                                    pe.matmul(dst, q_hh[:, bass.ds(tile * P, P)], k_hm[:, col:col + BANK],
                                              start=True, stop=False, skip_group_check=True)
                                    mm = edges(dst, tile, col // P, False)
                            mm.then_inc(c_scores, 1)

                    def product(pair, slot, first, last):
                        pe.wait_ge(c_values, n0 + pair * 2 + 2)
                        for q in range(4):
                            for odd in range(2):
                                mm = pe.matmul(ps[odd * D:(odd + 1) * D, N + q * BANK:N + (q + 1) * BANK],
                                               v_norm[:, slot + odd, :],
                                               probs_t[:, slot + odd, q * BANK:(q + 1) * BANK],
                                               start=first, stop=last)
                        mm.then_inc(c_product, 1)

                    def body(g, first):
                        scores(g, 0, first)
                        scores(g, 1, first)
                        if not first:
                            product(g * 2 - 1, 2, False, False)
                        scores(g, 2, first)
                        scores(g, 3, first)
                        product(g * 2, 0, first, False)

                    groups(pe, body)
                    product(2 * G - 1, 2, False, True)
                    for t in range(T):
                        if t % 4 == 0:
                            pe.wait_ge(c_prod_out, turn * 4 + t // 4 + 1)
                        mm = pe.matmul(ps[:, t * D:(t + 1) * D], halves[:, t * P:(t + 1) * P], fold[:],
                                       start=True, stop=True)
                    mm.then_inc(c_folded, 1)

                @block.scalar
                def _(act):
                    def body(g, first):
                        for k in range(GROUP):
                            tile = g * GROUP + k
                            for hf in range(2):
                                half = 2 * k + hf
                                if cosine:
                                    if not (first and half < 2):
                                        wait_apart(act, c_cos, m0 + g * (2 * GROUP) + (half - 1))
                                    rows = norm_row[:, hf * HALF:(hf + 1) * HALF]
                                    act.activation(relus[:, hf, :], rows, ACT.Ln, bias=cos_cols[:, 1:2],
                                                   scale=norms[:, bass.ds(tile, 1)]).then_inc(c_ln, 1)
                                    act.wait_ge(c_ln, m0 + g * (2 * GROUP) + (half + 1))
                                    act.activation(relus[:, hf, :], relus[:, hf, :], ACT.Exp,
                                                   scale=-1.0).then_inc(c_relu, 1)
                                else:
                                    act.wait_ge(c_scores, n0 * 2 + g * (2 * GROUP) + (half + 1))
                                    act.activation(relus[:, hf, :], ps[:, S0 + hf * HALF:S0 + (hf + 1) * HALF],
                                                   ACT.Relu, scale=1.0 / COL_SLOPE - 1.0).then_inc(c_relu, 1)
                            wait_apart(act, c_shift, n0 + g * GROUP + (k + 1))
                            act.activation(probs_t[:, k, :], probs_t[:, k, :], ACT.Exp,
                                           bias=shift[:, k % 2:k % 2 + 1],
                                           accum_out=denom[:, bass.ds(tile, 1)]).then_inc(c_probs, 1)
                    groups(act, body)
                    for q in range(4):
                        if q == 0:
                            act.wait_ge(c_product, p0 + T // 2)
                        act.activation(halves[:, q * BANK:(q + 1) * BANK], ps[:, N + q * BANK:N + (q + 1) * BANK],
                                       ACT.Copy).then_inc(c_prod_out, 1)

                @block.vector
                def _(dve):
                    def normalize(g, k):
                        tile = g * GROUP + k
                        dve.wait_ge(c_probs, n0 + g * GROUP + (k + 1))
                        dve.reciprocal(inv[:, bass.ds(tile, 1)], denom[:, bass.ds(tile, 1)]).then_inc(c_inv, 1)
                        dve.wait_ge(c_inv, n0 + g * GROUP + (k + 1))
                        dve.tensor_scalar(v_norm[:, k, :], v_head[:, tile, :], inv[:, bass.ds(tile, 1)], None,
                                          ALU.mult).then_inc(c_values, 1)

                    def body(g, first):
                        for k in range(GROUP):
                            for hf in range(2):
                                half = 2 * k + hf
                                dst = probs_t[:, k, hf * HALF:(hf + 1) * HALF]
                                if hf == 0 and not first:
                                    dve.wait_ge(c_product, p0 + g * 2 + (k // 2 - 1))
                                wait_apart(dve, c_relu, n0 * 2 + g * (2 * GROUP) + (half + 1))
                                if cosine:
                                    dve.wait_ge(c_scores, n0 * 2 + g * (2 * GROUP) + (half + 1))
                                    dve.scalar_tensor_tensor(dst, ps[:, S0:S0 + HALF], cos_cols[:, 0:1],
                                                             relus[:, hf, :], ALU.mult, ALU.mult).then_inc(c_cos, 1)
                                    wait_apart(dve, c_cos, m0 + g * (2 * GROUP) + (half + 1))
                                    dve.tensor_tensor_reduce(dst, ps[:, S0 + HALF:S0 + N], dst, 1.0, LOWEST,
                                                             ALU.add, ALU.max, rowmax[:, k % 2, hf:hf + 1]).then_inc(c_scaled, 1)
                                else:
                                    dve.tensor_tensor_reduce(dst, ps[:, S0 + hf * HALF:S0 + (hf + 1) * HALF],
                                                             relus[:, hf, :], COL_SLOPE, LOWEST, ALU.add, ALU.max,
                                                             rowmax[:, k % 2, hf:hf + 1]).then_inc(c_scaled, 1)
                            dve.wait_ge(c_scaled, n0 * 2 + g * (2 * GROUP) + (2 * k + 2))
                            dve.tensor_reduce(shift[:, k % 2:k % 2 + 1], rowmax[:, k % 2, :], AX, ALU.max,
                                              negate=True).then_inc(c_shift, 1)
                            if k >= 1:
                                normalize(g, k - 1)
                            elif not first:
                                normalize(g - 1, GROUP - 1)
                    groups(dve, body)
                    normalize(G - 1, GROUP - 1)
                    dve.wait_ge(c_folded, turn + 1)
                    dve.tensor_copy(mixed[:], ps[:, 0:T * D].rearrange("p (t d) -> p t d", t=T))

        c_ln = sem("c_ln")

        done = sem("done")
        stored = sem("stored")
        PER_NORM = 7

        def all_rows(v):
            return v.unsqueeze(2).to_broadcast([P, T, D])

        def layer_norm(dve, act, pool, at, src, scratch, dst):
            if dve is not None:
                dve.wait_ge(done, at)
                dve.tensor_reduce(stat_a[:], src, AX, ALU.add).then_inc(done, 1)
                dve.wait_ge(done, at + 1)
                dve.tensor_scalar(stat_a[:], stat_a[:], 1.0 / D, None, ALU.mult).then_inc(done, 1)
                dve.wait_ge(done, at + 2)
                dve.tensor_tensor(src, src, all_rows(stat_a[:]), ALU.subtract).then_inc(done, 1)
            if act is not None:
                act.wait_ge(done, at + 3)
                act.activation(scratch, src, ACT.Square).then_inc(done, 1)
            if dve is not None:
                dve.wait_ge(done, at + 4)
                dve.tensor_reduce(stat_b[:], scratch, AX, ALU.add).then_inc(done, 1)
                dve.wait_ge(done, at + 5)
                dve.tensor_scalar(stat_b[:], stat_b[:], 1.0 / D, EPS, ALU.mult, ALU.add).then_inc(done, 1)
            if pool is not None:
                pool.wait_ge(done, at + 6)
                pool.tensor_tensor(stat_b[:], stat_b[:], minus_half[:], ALU.pow).then_inc(done, 1)
            if dve is not None:
                dve.wait_ge(done, at + 7)
                dve.tensor_tensor(dst, src, all_rows(stat_b[:]), ALU.mult).then_inc(done, 1)
            return at + 8

        def elu(dve, act, at):
            if dve is not None:
                dve.wait_ge(done, at)
                dve.tensor_scalar(tmp_a[:], mixed[:], 0.0, None, ALU.min).then_inc(done, 1)
            if act is not None:
                act.wait_ge(done, at + 1)
                act.activation(tmp_b[:], mixed[:], ACT.Relu)
                act.activation(tmp_a[:], tmp_a[:], ACT.Exp).then_inc(done, 1)
            if dve is not None:
                dve.wait_ge(done, at + 2)
                dve.scalar_tensor_tensor(tmp_a[:], tmp_a[:], -1.0, tmp_b[:], ALU.add, ALU.add).then_inc(done, 1)
            return at + 3

        STEPS = (1 + 3 + 8 + 2 + 1 + 8, 3 + 1 + 8, 1 + 1 + 8, 1 + 8)
        PER_BATCH = sum(STEPS)

        def finish_layer(b, layer):
            base = b * PER_BATCH + sum(STEPS[:layer])
            X, H, A, Bt = nodes[:], mixed[:], tmp_a[:], tmp_b[:]
            G4 = gamma_row[:].unsqueeze(1).to_broadcast([P, T, D])
            B4 = beta_row[:].unsqueeze(1).to_broadcast([P, T, D])

            def steps(dve, act, pool, sp):
                at = base
                if layer == 0:
                    if dve is not None:
                        dve.tensor_tensor(H, H, values[:, :, D:2 * D], ALU.add).then_inc(done, 1)
                    at = elu(dve, act, at + 1)
                    at = layer_norm(dve, act, pool, at, A, Bt, A)
                    if dve is not None:
                        dve.wait_ge(done, at)
                        dve.tensor_tensor(A, A, G4, ALU.mult).then_inc(done, 1)
                        dve.wait_ge(done, at + 1)
                        dve.tensor_tensor(A, A, B4, ALU.add).then_inc(done, 1)
                    at = at + 2
                elif layer == 1:
                    at = elu(dve, act, at)
                elif layer == 2:
                    if dve is not None:
                        dve.scalar_tensor_tensor(A, H, GAT_SLOPE, H, ALU.mult, ALU.max).then_inc(done, 1)
                    at = at + 1
                if dve is not None:
                    if layer != 3:
                        dve.wait_ge(done, at)
                    dve.tensor_tensor(A, X, A if layer != 3 else H, ALU.add).then_inc(done, 1)
                at = layer_norm(dve, act, pool, at + 1, A, Bt, X)
                return at

            with nc.Block() as block:
                @block.vector
                def _(dve):
                    steps(dve, None, None, None)

                @block.scalar
                def _(act):
                    steps(None, act, None, None)

                @block.gpsimd
                def _(pool):
                    steps(None, None, pool, None)

                if layer == 3:
                    @block.sync
                    def _(sp):
                        sp.wait_ge(done, base + STEPS[3])
                        sp.dma_start(out[b].rearrange("(t p) d -> p t d", p=P), nodes[:]).then_inc(stored, 16)
                        wait_apart(sp, stored, b * 16 + 16)

        def clear_mixed():
            with nc.Block() as block:
                @block.vector
                def _(dve):
                    dve.memset(mixed[:], 0.0)

        def take_values():
            with nc.Block() as block:
                @block.scalar
                def _(act):
                    act.activation(v_head[:], values[:, :, 0:D], ACT.Copy)

        n_step = sem("n_step")
        diag_made = sem("diag_made")

        def cosine_operands(b):
            diag = spare
            with nc.Block() as block:
                @block.scalar
                def _(act):
                    act.activation(lines[:, 0, :], feat_t[:], ACT.Copy).then_inc(qk_copied, 1)
                    act.activation(lines[:, 1, :], feat_t[:], ACT.Copy).then_inc(qk_copied, 1)
                    act.activation(tmp_a[:], nodes[:], ACT.Square).then_inc(n_step, 1)
                    act.activation(v_head[:], nodes[:], ACT.Copy)

                @block.vector
                def _(dve):
                    dve.wait_ge(n_step, b * 3 + 1)
                    dve.tensor_reduce(stat_a[:], tmp_a[:], AX, ALU.add).then_inc(n_step, 1)
                    split_q_k(dve, (b * HEADS + b + HEADS) * 8, (b * HEADS + b + HEADS) * 2, lines[:, 0, :], lines[:, 1, :])
                    dve.wait_ge(n_step, b * 3 + 3)
                    for t in range(T):
                        dve.tensor_scalar(diag[:, t * P:(t + 1) * P], ident[:], norms[:, t:t + 1], None,
                                          ALU.mult).then_inc(diag_made, 1)
                    for q in range(4):
                        dve.wait_ge(diag_made, b * (T + 4) + T + q + 1)
                        if q == 0:
                            dve.wait_ge(qk_split, (b * HEADS + b + HEADS + 1) * 8)
                        dve.tensor_copy(norm_row[:, q * BANK:(q + 1) * BANK], ps[:, q * BANK:(q + 1) * BANK])

                @block.gpsimd
                def _(pool):
                    pool.wait_ge(n_step, b * 3 + 2)
                    pool.tensor_tensor(norms[:], stat_a[:], plus_half[:], ALU.pow).then_inc(n_step, 1)

                @block.tensor
                def _(pe):
                    for q in range(4):
                        if q == 0:
                            pe.wait_ge(diag_made, b * (T + 4) + T)
                        pe.matmul(ps[:, q * BANK:(q + 1) * BANK], ones[:], diag[:, q * BANK:(q + 1) * BANK],
                                  start=True, stop=True).then_inc(diag_made, 1)

        with nc.Fori(0, B) as b:
            load(b)
            transpose_nodes(b * 4)
            line_operands(b * 2, 0)
            node_values(b * 3, 2 * D, w0_sb, None)
            take_values()
            attention_rows(b * (1 + HEADS), [(q_hh, k_hm)], False)
            finish_layer(b, 0)
            transpose_nodes(b * 4 + 1)
            line_operands(b * 2 + 1, 2)
            node_values(b * 3 + 1, D, w1_sb, b1_row)
            take_values()
            attention_columns(b, False)
            finish_layer(b, 1)
            transpose_nodes(b * 4 + 2)
            node_values(b * 3 + 2, C, wv_sb, bv_row)
            clear_mixed()
            with nc.Fori(0, HEADS) as h:
                head_operands(b, h)
                attention_rows(b * (1 + HEADS) + h + 1,
                               [(q_hh, k_hm), (q_mm, k_hm), (q_hl, k_lh)], True)
            finish_layer(b, 2)
            transpose_nodes(b * 4 + 3)
            cosine_operands(b)
            attention_columns(b, True)
            finish_layer(b, 3)


def kernel(x, adj, L0_gnn_W, L0_gnn_a, L0_gnn_W_res, L0_gnn_gamma, L0_gnn_beta, L1_gnn_W1, L1_gnn_b1, L1_gnn_a1,
           L1_gnn_ba1, L1_gnn_a2, L1_gnn_ba2, L2_gnn_Wv, L2_gnn_bv, L2_gnn_Wq, L2_gnn_bq, L2_gnn_Wk, L2_gnn_bk,
           L3_gnn_beta, L3_gnn_bias):
    import numpy as np
    import concourse.bacc as bacc
    from concourse.bass_utils import run_bass_kernel_spmd

    def flat(a):
        return np.ascontiguousarray(np.asarray(a))

    a0 = flat(L0_gnn_a)
    arrays = {
        "x": flat(x), "adj": flat(adj),
        "w0": np.concatenate([flat(L0_gnn_W), flat(L0_gnn_W_res)], axis=1),
        "w0_t": flat(flat(L0_gnn_W).T),
        "a0": flat(a0.reshape(2, -1).T),
        "gamma": flat(L0_gnn_gamma)[None], "beta": flat(L0_gnn_beta)[None],
        "w1": flat(L1_gnn_W1), "w1_t": flat(flat(L1_gnn_W1).T),
        "b1": flat(L1_gnn_b1)[None],
        "a1": flat(L1_gnn_a1)[:, None], "ba1": flat(L1_gnn_ba1)[None],
        "a2": flat(L1_gnn_a2)[:, None], "ba2": flat(L1_gnn_ba2)[None],
        "wv": flat(flat(L2_gnn_Wv).transpose(1, 0, 2).reshape(64, -1)), "bv": flat(L2_gnn_bv).reshape(1, -1),
        "wq": flat(flat(L2_gnn_Wq).transpose(1, 0, 2)), "bq": flat(flat(L2_gnn_bq).T),
        "wk": flat(flat(L2_gnn_Wk).transpose(1, 0, 2)), "bk": flat(flat(L2_gnn_bk).T),
        "cos_beta": flat(L3_gnn_beta)[None], "cos_bias": flat(L3_gnn_bias)[None],
    }
    arrays = {k: flat(a) for k, a in arrays.items()}
    nc = bacc.Bacc("TRN2", target_bir_lowering=False, num_devices=1)
    args = [nc.dram_tensor(f"in_{n}", a.shape, mybir.dt.from_np(a.dtype), kind="ExternalInput").ap()
            for n, a in arrays.items()]
    out = nc.dram_tensor("out", arrays["x"].shape, F32, kind="ExternalOutput").ap()
    build(nc, *args, out)
    r = run_bass_kernel_spmd(nc, [{f"in_{n}": a for n, a in arrays.items()}], core_ids=[0])
    return r.results[0]["out"]
```

```python
from contextlib import ExitStack

import concourse.bass as bass
from concourse import mybir

F32 = mybir.dt.float32
BF16 = mybir.dt.bfloat16
I32 = mybir.dt.int32
ALU = mybir.AluOpType
ACT = mybir.ActivationFunctionType
AX = mybir.AxisListType.X

P = 128
BANK = 512
NO_EDGE = 9.0e15
LOWEST = -3.0e38
GAT_SLOPE = 0.2
COL_SLOPE = 0.01
EPS = 1e-5
HEADS = 4


def build(nc, x, adj, w0, w0_t, a0, gamma, beta, w1, w1_t, b1, a1, ba1, a2, ba2,
          wv, bv, wq, bq, wk, bk, cos_beta, cos_bias, out):
    B, N, D = x.shape
    T = N // P
    GROUP = BANK // P
    G = T // GROUP
    HALF = N // 2
    C = HEADS * D
    assert D * 2 == P and T == GROUP * G and N == 4 * BANK

    ctx = ExitStack()
    with ctx:
        def sb(name, shape, dt=F32):
            return ctx.enter_context(nc.sbuf_tensor(name, shape, dt))

        def sem(name):
            return ctx.enter_context(nc.semaphore(name))

        mask = sb("mask", [P, T, N], BF16)
        turned = sb("turned", [P, 2, T, 2 * P])
        probs = sb("probs", [P, 2, N])
        relus = sb("relus", [P, 4, HALF])
        feat_t = sb("feat_t", [P, N])
        q_hh = sb("q_hh", [P, N], BF16)
        q_mm = sb("q_mm", [P, N], BF16)
        q_hl = sb("q_hl", [P, N], BF16)
        k_hm = sb("k_hm", [P, N], BF16)
        k_lh = sb("k_lh", [P, N], BF16)
        values = sb("values", [P, T, C])
        v_head = sb("v_head", [P, T, D])
        nodes = sb("nodes", [P, T, D])
        mixed = sb("mixed", [P, T, D])
        part = sb("part", [P, 2, 2, D])
        denom = sb("denom", [P, T])
        inv = sb("inv", [P, T])
        rowmax = sb("rowmax", [P, 2, 4])
        shift = sb("shift", [P, 2])
        folded_in = sb("folded_in", [P, 2 * P])
        stat_a = sb("stat_a", [P, T])
        stat_b = sb("stat_b", [P, T])
        root = sb("root", [P, T])
        norms = sb("norms", [P, T])
        ident = sb("ident", [P, P])
        ident_b = sb("ident_b", [P, P], BF16)
        fold = sb("fold", [P, D])
        ones = sb("ones", [P, P])
        plus_half = sb("plus_half", [P, T])
        w0_sb = sb("w0_sb", [P, 2 * D + 2])
        w1_sb = sb("w1_sb", [P, D + 2])
        wv_sb = sb("wv_sb", [P, C])
        wq_sb = sb("wq_sb", [P, HEADS, P])
        wk_sb = sb("wk_sb", [P, HEADS, P])
        wq_h = sb("wq_h", [P, P])
        wk_h = sb("wk_h", [P, P])
        w0t_sb = sb("w0t_sb", [D, D])
        w1t_sb = sb("w1t_sb", [D, D])
        a_cols = sb("a_cols", [D, 4])
        b1_col = sb("b1_col", [D, 1])
        b1_wide = sb("b1_wide", [D, P])
        ba_cols = sb("ba_cols", [P, 2])
        line_bias = sb("line_bias", [P, 4])
        b1_row = sb("b1_row", [P, D])
        bv_row = sb("bv_row", [P, C])
        gamma_row = sb("gamma_row", [P, D])
        beta_row = sb("beta_row", [P, D])
        bq_col = sb("bq_col", [P, HEADS])
        bk_col = sb("bk_col", [P, HEADS])
        cos_cols = sb("cos_cols", [P, 2])
        line = sb("line", [P, 2, T])
        line_hi = sb("line_hi", [P, 2, T], BF16)
        adj_in = values[:, :, :].rearrange("p t c -> p (t c)").rearrange("p (s n) -> p s n", s=2).bitcast(I32)
        probs_t = turned[:, :, :, :].rearrange("p s a b -> p (s a b)").rearrange("p (s n) -> p s n", s=GROUP)
        lines = probs
        twice = probs[:, 0, :].rearrange("p (t e) -> p t e", t=T)
        halves = probs[:, 0, :]
        norm_row = probs[:, 1, :]
        v_norm = folded_in[:, 0:GROUP * D].rearrange("p (s d) -> p s d", s=GROUP)
        recips = relus[:, :, :].rearrange("p a b -> p (a b)").rearrange("p (s n) -> p s n", s=2)
        tmp_a = relus[:, 0, :].rearrange("p (t d) -> p t d", t=T)
        tmp_b = relus[:, 1, :].rearrange("p (t d) -> p t d", t=T)
        diag = relus[:, 2:4, :].rearrange("p a b -> p (a b)")
        line_cols = probs[:, 1, :].bitcast(BF16).rearrange("p (r t c) -> p r t c", r=2, t=T)

        ps = ctx.enter_context(nc.psum_tensor("ps", [P, 8 * BANK], F32))
        S0, T0, O0, F0, C0 = 0, N, N + 2 * BANK, N + 3 * BANK, N

        r_scores = sem("r_scores")
        r_relu = sem("r_relu")
        r_scaled = sem("r_scaled")
        r_shift = sem("r_shift")
        r_probs = sem("r_probs")
        r_turned = sem("r_turned")
        r_evac_dve = sem("r_evac_dve")
        r_evac_act = sem("r_evac_act")
        r_product = sem("r_product")
        r_prod_out = sem("r_prod_out")
        r_folded = sem("r_folded")
        r_inv = sem("r_inv")
        r_mixed = sem("r_mixed")
        r_lrn = sem("r_lrn")

        landed = sem("landed")
        zeroed = sem("zeroed")
        made = sem("made")
        loads = [
            (w0_sb[0:D, 0:2 * D], w0), (w1_sb[0:D, 0:D], w1), (wv_sb[0:D, :], wv),
            (wq_sb[0:D, :, 0:D], wq), (wq_sb[0:D, :, D:P], wq),
            (wk_sb[0:D, :, 0:D], wk), (wk_sb[0:D, :, D:P], wk),
            (w0t_sb[:, :], w0_t), (w1t_sb[:, :], w1_t),
            (a_cols[:, 0:2], a0), (a_cols[:, 2:3], a1), (a_cols[:, 3:4], a2), (b1_col[:, :], b1.rearrange("a d -> d a")),
            (ba_cols[:, 0:1], ba1.to_broadcast([P, 1])), (ba_cols[:, 1:2], ba2.to_broadcast([P, 1])),
            (b1_row[:, :], b1.to_broadcast([P, D])), (bv_row[:, :], bv.to_broadcast([P, C])),
            (gamma_row[:, :], gamma.to_broadcast([P, D])), (beta_row[:, :], beta.to_broadcast([P, D])),
            (bq_col[0:D, :], bq), (bq_col[D:P, :], bq), (bk_col[0:D, :], bk), (bk_col[D:P, :], bk),
            (cos_cols[:, 0:1], cos_beta.to_broadcast([P, 1])), (cos_cols[:, 1:2], cos_bias.to_broadcast([P, 1])),
        ]
        with nc.Block() as block:
            @block.sync
            def _(sp):
                sp.wait_ge(zeroed, 7)
                for dst, src in loads:
                    sp.dma_start(dst, src).then_inc(landed, 16)

            @block.gpsimd
            def _(pool):
                for t in (w0_sb, w1_sb, wv_sb, wq_sb, wk_sb, ident, line_bias):
                    pool.memset(t[:], 0.0).then_inc(zeroed, 1)
                pool.memset(ones[:], 1.0)
                pool.memset(plus_half[:], 0.5)
                pool.wait_ge(zeroed, 7)
                pool.affine_select(out=ident[:], in_=ident[:], compare_op=ALU.not_equal, fill=1.0, base=0,
                                   pattern=[[-1, P]], channel_multiplier=1).then_inc(made, 1)

            @block.vector
            def _(dve):
                dve.wait_ge(made, 1)
                dve.tensor_copy(ident_b[:], ident[:]).then_inc(made, 1)
                dve.tensor_tensor(fold[:], ident[:, 0:D], ident[:, D:P], ALU.add).then_inc(made, 1)
                dve.wait_ge(landed, 16 * len(loads))
                dve.tensor_copy(b1_wide[:], b1_col[:].to_broadcast([D, P])).then_inc(made, 1)
                dve.tensor_scalar(bq_col[:], bq_col[:], float(D) ** -0.5, None, ALU.mult).then_inc(made, 1)

            @block.tensor
            def _(pe):
                pe.wait_ge(made, 5)
                pe.wait_ge(landed, 16 * len(loads))
                for c, wt in enumerate((w0t_sb, w1t_sb)):
                    pe.matmul(ps[0:D, 2 * c:2 * c + 2], wt[:], a_cols[:, 2 * c:2 * c + 2],
                              start=True, stop=True).then_inc(made, 1)
                for c in range(2):
                    pe.matmul(ps[:, BANK + c:BANK + c + 1], b1_wide[:], a_cols[:, 2 + c:3 + c],
                              start=True, stop=True).then_inc(made, 1)

            @block.scalar
            def _(act):
                act.preload_act_table_set("natural_log_exp_and_others")
                act.wait_ge(made, 9)
                act.activation(w0_sb[0:D, 2 * D:2 * D + 2], ps[0:D, 0:2], ACT.Copy)
                act.activation(w1_sb[0:D, D:D + 2], ps[0:D, 2:4], ACT.Copy)
                for c in range(2):
                    act.activation(line_bias[:, 2 + c:3 + c], ps[:, BANK + c:BANK + c + 1], ACT.Identity,
                                   bias=ba_cols[:, c:c + 1])

        bounds = {}

        def wait_apart(eng, semaphore, value):
            if eng.engine not in bounds:
                bounds[eng.engine] = eng.alloc_register(f"bound_{len(bounds)}")
            bound = bounds[eng.engine]
            eng.reg_mov(bound, value)
            eng.wait_ge(made, 1)
            eng.wait_ge(semaphore, bound)

        x_landed = sem("x_landed")
        adj_landed = [sem(f"adj_landed{s}") for s in range(2)]
        adj_used = sem("adj_used")

        def adj_rows(sp, b, tile, slot):
            rows = adj.rearrange("b (t p) j -> b t p j", p=P)
            sp.dma_start(adj_in[:, slot, :], rows[b, tile]).then_inc(adj_landed[slot], 16)

        def load(b):
            with nc.Block() as block:
                @block.sync
                def _(sp):
                    sp.dma_start(nodes[:], x[b].rearrange("(t p) d -> p t d", p=P)).then_inc(x_landed, 16)
                    for slot in range(2):
                        adj_rows(sp, b, slot, slot)
                    wait_apart(sp, x_landed, b * 16 + 16)

        def load_adjacency(sp, b):
            with sp.Fori(1, T // 2) as pair:
                for slot in range(2):
                    sp.wait_ge(adj_used, b * T + pair * 2 + (slot - 1))
                    adj_rows(sp, b, pair * 2 + slot, slot)

        def make_mask(dve, b, g, k):
            dve.wait_ge(adj_landed[k % 2], b * (8 * T) + g * (8 * GROUP) + 16 * (k // 2 + 1))
            dve.tensor_scalar(mask[:, g * GROUP + k, :], adj_in[:, k % 2, :], 1.0, NO_EDGE,
                              ALU.subtract, ALU.mult).then_inc(adj_used, 1)

        doubled = sem("doubled")
        xt_ready = sem("xt_ready")
        xt_copied = sem("xt_copied")

        def transpose_nodes(turn):
            with nc.Block() as block:
                @block.gpsimd
                def _(pool):
                    pool.tensor_scalar(twice[:, :, D:P], nodes[:], 1.0, 0.0, ALU.mult, ALU.add).then_inc(doubled, 1)

                @block.vector
                def _(dve):
                    dve.tensor_copy(twice[:, :, 0:D], nodes[:]).then_inc(doubled, 1)
                    for q in (1, 3):
                        dve.wait_ge(xt_ready, turn * 4 + q + 1)
                        dve.tensor_copy(feat_t[:, q * BANK:(q + 1) * BANK], ps[:, q * BANK:(q + 1) * BANK])

                @block.tensor
                def _(pe):
                    pe.wait_ge(doubled, turn * 2 + 2)
                    for t in range(T):
                        mm = pe.transpose(ps[:, t * P:(t + 1) * P], twice[:, t, :], ident[:])
                        if t % 4 == 3:
                            mm.then_inc(xt_ready, 1)

                @block.scalar
                def _(act):
                    for q in (0, 2):
                        act.wait_ge(xt_ready, turn * 4 + q + 1)
                        act.activation(feat_t[:, q * BANK:(q + 1) * BANK], ps[:, q * BANK:(q + 1) * BANK], ACT.Copy)

        v_ready = sem("v_ready")
        line_step = sem("line_step")
        cols_zeroed = sem("cols_zeroed")
        cols_turned = sem("cols_turned")

        def node_operands(turn, layer):
            weights, stride, at = ((w0_sb, 2 * P, 2 * D), (w1_sb, P, D))[layer]
            with nc.Block() as block:
                @block.gpsimd
                def _(pool):
                    zero = line_cols[:, :, :, :].rearrange("p r t c -> p (r t c)").bitcast(F32)
                    pool.memset(zero, 0.0).then_inc(cols_zeroed, 1)
                    wait_apart(pool, cols_zeroed, turn * 3 + 1)
                    pool.memset(line_cols[:, 0, :, 3:6], 1.0).then_inc(cols_zeroed, 1)
                    pool.memset(line_cols[:, 1, :, 0:3], 1.0).then_inc(cols_zeroed, 1)

                @block.tensor
                def _(pe):
                    for t in range(T):
                        mm = pe.matmul(ps[:, t * stride:t * stride + at + 2], feat_t[:, t * P:(t + 1) * P],
                                       weights[:, 0:at + 2], start=True, stop=True)
                    mm.then_inc(v_ready, 1)
                    pe.wait_ge(cols_zeroed, turn * 3 + 3)
                    pe.wait_ge(line_step, turn * 8 + 8)
                    for r in range(2):
                        for t in range(T):
                            mm = pe.transpose(ps[:, r * HALF:(r + 1) * HALF].bitcast(BF16)[:, t * P:(t + 1) * P],
                                              line_cols[:, r, t, :], ident_b[:])
                        mm.then_inc(cols_turned, 1)

                @block.vector
                def _(dve):
                    products = ps[:, 0:T * stride].rearrange("p (t c) -> p t c", t=T)
                    dve.wait_ge(v_ready, turn + 1)
                    for r in range(2):
                        dve.tensor_scalar(line[:, r, :], products[:, :, at + r], line_bias[:, 2 * layer + r:2 * layer + r + 1],
                                          None, ALU.add).then_inc(line_step, 1)
                    if layer == 0:
                        dve.tensor_copy(mixed[:], products[:, :, D:2 * D]).then_inc(line_step, 1)
                        dve.tensor_copy(v_head[:], products[:, :, 0:D])
                    else:
                        dve.tensor_tensor(v_head[:], products[:, :, 0:D], b1_row[:].unsqueeze(1).to_broadcast([P, T, D]),
                                          ALU.add).then_inc(line_step, 1)
                    dve.wait_ge(line_step, turn * 8 + 3)
                    dve.wait_ge(cols_zeroed, turn * 3 + 3)

                    def parts(n):
                        dve.tensor_copy(line_cols[:, 0, :, n], line_hi[:, 0, :])
                        return dve.tensor_copy(line_cols[:, 1, :, 3 + n], line_hi[:, 1, :])
                    for n in range(2):
                        dve.tensor_copy(line_hi[:], line[:]).then_inc(line_step, 1)
                        dve.wait_ge(line_step, turn * 8 + (4 + 2 * n))
                        parts(n)
                        dve.tensor_tensor(line[:], line[:], line_hi[:], ALU.subtract).then_inc(line_step, 1)
                        dve.wait_ge(line_step, turn * 8 + (5 + 2 * n))
                    dve.tensor_copy(line_cols[:, 0, :, 2], line[:, 0, :])
                    dve.tensor_copy(line_cols[:, 1, :, 5], line[:, 1, :]).then_inc(line_step, 1)
                    wait_apart(dve, cols_turned, turn * 2 + 2)
                    dve.tensor_copy(k_hm[:], ps[:, HALF:N].bitcast(BF16))

                @block.scalar
                def _(act):
                    act.wait_ge(cols_turned, turn * 2 + 1)
                    act.activation(q_hh[:], ps[:, 0:HALF].bitcast(BF16), ACT.Copy)

        values_ready = sem("values_ready")

        def head_values(b):
            with nc.Block() as block:
                @block.tensor
                def _(pe):
                    for t in range(T):
                        mm = pe.matmul(ps[:, t * C:(t + 1) * C], feat_t[:, t * P:(t + 1) * P], wv_sb[:],
                                       start=True, stop=True)
                        if t % 4 == 3:
                            mm.then_inc(values_ready, 1)

                @block.vector
                def _(dve):
                    dve.memset(mixed[:], 0.0)
                    for q in range(4):
                        dve.wait_ge(values_ready, b * 4 + (q + 1))
                        dve.tensor_tensor(values[:, 4 * q:4 * q + 4, :],
                                          ps[:, q * 4 * C:(q + 1) * 4 * C].rearrange("p (t c) -> p t c", t=4),
                                          bv_row[:].unsqueeze(1).to_broadcast([P, 4, C]), ALU.add)

        picked = sem("picked")
        qk_ready = sem("qk_ready")
        qk_copied = sem("qk_copied")
        qk_split = sem("qk_split")

        def split_q_k(dve, base, copied_base, q, k):
            lo, up = slice(0, D), slice(D, P)
            dve.wait_ge(qk_copied, copied_base + 1)
            dve.tensor_copy(q_hh[:], q).then_inc(qk_split, 1)
            dve.wait_ge(qk_split, base + 1)
            dve.tensor_tensor(q, q, q_hh[:], ALU.subtract).then_inc(qk_split, 1)
            dve.tensor_copy(q_hl[lo, :], q_hh[lo, :])
            dve.wait_ge(qk_split, base + 2)
            dve.tensor_copy(q_mm[:], q).then_inc(qk_split, 1)
            dve.wait_ge(qk_split, base + 3)
            dve.tensor_tensor(q_hl[up, :], q[up, :], q_mm[up, :], ALU.subtract)
            dve.wait_ge(qk_copied, copied_base + 2)
            dve.tensor_copy(k_hm[:], k).then_inc(qk_split, 1)
            dve.wait_ge(qk_split, base + 4)
            dve.tensor_copy(k_lh[up, :], k_hm[up, :]).then_inc(qk_split, 1)
            dve.tensor_tensor(k, k, k_hm[:], ALU.subtract).then_inc(qk_split, 1)
            dve.wait_ge(qk_split, base + 6)
            dve.tensor_copy(k_hm[up, :], k[up, :])
            dve.tensor_copy(k_lh[lo, :], k[lo, :]).then_inc(qk_split, 1)
            dve.wait_ge(qk_split, base + 7)
            dve.tensor_tensor(k_lh[lo, :], k[lo, :], k_lh[lo, :], ALU.subtract).then_inc(qk_split, 1)

        def head_operands(b, h):
            turn = b * HEADS + h
            with nc.Block() as block:
                @block.scalar
                def _(act):
                    act.activation(wq_h[:], wq_sb[:, h, :], ACT.Copy).then_inc(picked, 1)
                    act.activation(wk_h[:], wk_sb[:, h, :], ACT.Copy).then_inc(picked, 1)
                    act.activation(v_head[:], values[:, :, bass.ds(h * D, D)], ACT.Copy)
                    wait_apart(act, qk_ready, turn * 2 + 1)
                    act.activation(lines[:, 0, :], ps[:, 0:N], ACT.Identity, bias=bq_col[:, bass.ds(h, 1)],
                                   scale=float(D) ** -0.5).then_inc(qk_copied, 1)
                    wait_apart(act, qk_ready, turn * 2 + 2)
                    act.activation(lines[:, 1, :], ps[:, N:2 * N], ACT.Identity,
                                   bias=bk_col[:, bass.ds(h, 1)]).then_inc(qk_copied, 1)

                @block.tensor
                def _(pe):
                    for r, w in enumerate((wq_h, wk_h)):
                        pe.wait_ge(picked, turn * 2 + r + 1)
                        for q in range(4):
                            c = r * N + q * BANK
                            mm = pe.matmul(ps[:, c:c + BANK], w[:], feat_t[:, q * BANK:(q + 1) * BANK],
                                           start=True, stop=True)
                        mm.then_inc(qk_ready, 1)

                @block.vector
                def _(dve):
                    split_q_k(dve, (turn + b) * 8, (turn + b) * 2, lines[:, 0, :], lines[:, 1, :])

        def attention_rows(turn, passes, weight, loading=None):
            n0 = turn * T
            p0 = turn * (T // 2)

            def groups(eng, body):
                body(0, True, False)
                with eng.Fori(1, G - 1) as g:
                    body(g, False, False)
                body(G - 1, False, True)

            with nc.Block() as block:
                if loading is not None:
                    @block.sync
                    def _(sp):
                        load_adjacency(sp, loading)

                @block.tensor
                def _(pe):
                    def scores(g, k, hf, free):
                        if not free:
                            pe.wait_ge(r_scaled, n0 * 2 + g * (2 * GROUP) + (2 * k + hf - 1))
                        tile = g * GROUP + k
                        if hf == 0 and loading is not None:
                            pe.wait_ge(adj_used, loading * T + g * GROUP + (k + 1))
                        for q in range(2):
                            col = hf * HALF + q * BANK
                            dst = ps[:, S0 + col:S0 + col + BANK]
                            for n, (a, c) in enumerate(passes):
                                pe.matmul(dst, a[:, bass.ds(tile * P, P)], c[:, col:col + BANK],
                                          start=(n == 0), stop=False)
                            mm = pe.matmul(dst, ident_b[:], mask[:, tile, col:col + BANK],
                                           start=False, stop=True)
                        mm.then_inc(r_scores, 1)

                    def transposes(g, k, chunks, first):
                        for c in chunks:
                            if c == 0:
                                pe.wait_ge(r_probs, n0 + g * GROUP + (k + 1))
                            if not (first and k == 0 and c < 2):
                                pe.wait_ge((r_evac_dve, r_evac_act)[c % 2], n0 * 2 + g * (2 * GROUP) + (2 * k + c // 2))
                            bank = T0 + (c % 2) * BANK
                            for u in range(4):
                                j = 4 * c + u
                                mm = pe.transpose(ps[:, bank + u * P:bank + (u + 1) * P],
                                                  probs[:, k % 2, j * P:(j + 1) * P], ident[:])
                            mm.then_inc(r_turned, 1)

                    def product(g, s, quarters, first):
                        for c in quarters:
                            if c == 0:
                                pe.wait_ge(r_evac_act, n0 * 2 + g * (2 * GROUP) + 4 * (s + 1))
                                pe.wait_ge(r_evac_dve, n0 * 2 + g * (2 * GROUP) + 4 * (s + 1))
                                if not (first and s == 0):
                                    pe.wait_ge(r_prod_out, p0 + g * 2 + s)
                            for j in range(4 * c, 4 * c + 4):
                                half = (j % 2) * D
                                mm = pe.matmul(ps[half:half + D, O0:O0 + 2 * P], v_head[:, j, :], turned[:, s, j, :],
                                               start=(j < 2), stop=(j >= T - 2))
                        if quarters[-1] == 3:
                            mm.then_inc(r_product, 1)

                    def turn_product(g, s, first):
                        pe.wait_ge(r_prod_out, p0 + g * 2 + (s + 1))
                        if not (first and s == 0):
                            pe.wait_ge(r_mixed, p0 + g * 2 + s)
                        for k in range(2):
                            mm = pe.transpose(ps[:, F0 + k * P:F0 + (k + 1) * P], folded_in[:, k * P:(k + 1) * P],
                                              ident[:])
                        mm.then_inc(r_folded, 1)

                    def body(g, first, last, second=False):
                        for k in range(GROUP):
                            more = not (last and k >= GROUP - 2)
                            pair = (g, 0) if k >= 2 else (g - 1, 1)
                            busy = k >= 2 or not first
                            if more:
                                scores(g, k + 2, 0, False)
                            transposes(g, k, (0, 1), first)
                            if k % 2 == 0 and not first:
                                turn_product(g - 1, k // 2, second)
                            if busy:
                                product(*pair, (2 * (k % 2),), first)
                            if more:
                                scores(g, k + 2, 1, False)
                            transposes(g, k, (2, 3), first)
                            if busy:
                                product(*pair, (2 * (k % 2) + 1,), first)

                    for k in range(2):
                        for hf in range(2):
                            scores(0, k, hf, k == 0)
                    body(0, True, False)
                    body(1, False, False, True)
                    with pe.Fori(2, G - 1) as g:
                        body(g, False, False)
                    body(G - 1, False, True)
                    turn_product(G - 1, 0, False)
                    product(G - 1, 1, (0, 1, 2, 3), False)
                    turn_product(G - 1, 1, False)

                @block.scalar
                def _(act):
                    def evacuate(g, k, c, first):
                        act.wait_ge(r_turned, n0 * 4 + g * (4 * GROUP) + (4 * k + c + 1))
                        if k % 2 == 0 and c == 1 and not first:
                            act.wait_ge(r_product, p0 + g * 2 + (k // 2 - 1))
                        act.activation(turned[:, k // 2, 4 * c:4 * c + 4, (k % 2) * P:(k % 2 + 1) * P],
                                       ps[:, T0 + BANK:T0 + 2 * BANK].rearrange("p (a b) -> p a b", a=4),
                                       ACT.Copy).then_inc(r_evac_act, 1)

                    def copy_product(g, s, first):
                        act.wait_ge(r_product, p0 + g * 2 + (s + 1))
                        if not (first and s == 0):
                            act.wait_ge(r_folded, p0 + g * 2 + s)
                        act.activation(folded_in[:], ps[:, O0:O0 + 2 * P], ACT.Copy).then_inc(r_prod_out, 1)

                    def relu(g, k, hf):
                        act.wait_ge(r_scores, n0 * 2 + g * (2 * GROUP) + (2 * k + hf + 1))
                        act.activation(relus[:, hf, :], ps[:, S0 + hf * HALF:S0 + (hf + 1) * HALF],
                                       ACT.Relu, scale=1.0 / GAT_SLOPE - 1.0).then_inc(r_relu, 1)

                    def exp(g, k):
                        wait_apart(act, r_shift, n0 + g * GROUP + (k + 1))
                        act.activation(probs[:, k % 2, :], probs[:, k % 2, :], ACT.Exp,
                                       bias=shift[:, k % 2:k % 2 + 1],
                                       accum_out=denom[:, bass.ds(g * GROUP + k, 1)]).then_inc(r_probs, 1)

                    def body(g, first, last, second=False):
                        for k in range(GROUP):
                            more = not (last and k >= GROUP - 2)
                            if k % 2 == 0 and not first:
                                copy_product(g - 1, k // 2, second)
                            if more:
                                relu(g, k + 2, 0)
                            evacuate(g, k, 1, first)
                            if not (last and k == GROUP - 1):
                                exp(g, k + 1)
                            if more:
                                relu(g, k + 2, 1)
                            evacuate(g, k, 3, first)

                    relu(0, 0, 0)
                    relu(0, 0, 1)
                    exp(0, 0)
                    relu(0, 1, 0)
                    relu(0, 1, 1)
                    body(0, True, False)
                    body(1, False, False, True)
                    with act.Fori(2, G - 1) as g:
                        body(g, False, False)
                    body(G - 1, False, True)
                    copy_product(G - 1, 0, False)
                    copy_product(G - 1, 1, False)

                @block.vector
                def _(dve):
                    def leaky(g, k, hf, free):
                        if not free:
                            dve.wait_ge(r_turned, n0 * 4 + g * (4 * GROUP) + (4 * k - 6 + 2 * hf))
                        wait_apart(dve, r_relu, n0 * 2 + g * (2 * GROUP) + (2 * k + hf + 1))
                        dve.tensor_tensor_reduce(
                            probs[:, k % 2, hf * HALF:(hf + 1) * HALF], ps[:, S0 + hf * HALF:S0 + (hf + 1) * HALF],
                            relus[:, hf, :], GAT_SLOPE, LOWEST, ALU.add, ALU.max,
                            rowmax[:, k % 2, hf:hf + 1]).then_inc(r_scaled, 1)
                        if hf == 1:
                            dve.wait_ge(r_scaled, n0 * 2 + g * (2 * GROUP) + (2 * k + 2))
                            dve.tensor_reduce(shift[:, k % 2:k % 2 + 1], rowmax[:, k % 2, 0:2], AX, ALU.max,
                                              negate=True).then_inc(r_shift, 1)

                    def evacuate(g, k, c, first):
                        dve.wait_ge(r_turned, n0 * 4 + g * (4 * GROUP) + (4 * k + c + 1))
                        if k % 2 == 0 and c == 0 and not first:
                            dve.wait_ge(r_product, p0 + g * 2 + (k // 2 - 1))
                        dve.tensor_copy(turned[:, k // 2, 4 * c:4 * c + 4, (k % 2) * P:(k % 2 + 1) * P],
                                        ps[:, T0:T0 + BANK].rearrange("p (a b) -> p a b", a=4)).then_inc(r_evac_dve, 1)

                    def mix(g, s):
                        tile = g * GROUP + 2 * s
                        pair = p0 * 2 + g * 4 + 2 * s
                        dve.wait_ge(r_probs, n0 + g * GROUP + 2 * (s + 1))
                        zs = inv[:, bass.ds(tile, 2)]
                        dve.reciprocal(zs, denom[:, bass.ds(tile, 2)]).then_inc(r_inv, 1)
                        dve.wait_ge(r_folded, p0 + g * 2 + (s + 1))
                        prod = ps[:, F0:F0 + 2 * P].rearrange("p (k h d) -> p k d h", k=2, h=2)
                        dve.tensor_reduce(part[:, s], prod, AX, ALU.add).then_inc(r_mixed, 1)
                        dve.wait_ge(r_inv, pair + 1)
                        dve.wait_ge(r_mixed, p0 + g * 2 + (s + 1))
                        dve.tensor_tensor(part[:, s], part[:, s], zs.unsqueeze(2).to_broadcast([P, 2, D]),
                                          ALU.mult).then_inc(r_inv, 1)
                        dst = mixed[:, bass.ds(tile, 2), :]
                        dve.wait_ge(r_inv, pair + 2)
                        dve.scalar_tensor_tensor(dst, part[:, s], weight, dst, ALU.mult, ALU.add)

                    def body(g, first, last):
                        for k in range(GROUP):
                            more = not (last and k >= GROUP - 2)
                            evacuate(g, k, 0, first)
                            if k % 2 == 0 and not first:
                                mix(g - 1, k // 2)
                            if loading is not None and not (last and k > 0):
                                make_mask(dve, loading, g, k + 3)
                            if more:
                                leaky(g, k + 2, 0, False)
                            evacuate(g, k, 2, first)
                            if more:
                                leaky(g, k + 2, 1, False)

                    if loading is not None:
                        make_mask(dve, loading, 0, 0)
                        make_mask(dve, loading, 0, 1)
                    for k in range(2):
                        for hf in range(2):
                            leaky(0, k, hf, True)
                        if k == 0 and loading is not None:
                            make_mask(dve, loading, 0, 2)
                    groups(dve, body)
                    mix(G - 1, 0)
                    mix(G - 1, 1)

        c_scores = sem("c_scores")
        c_relu = sem("c_relu")
        c_ln = sem("c_ln")
        c_recip = sem("c_recip")
        c_cos = sem("c_cos")
        c_scaled = sem("c_scaled")
        c_shift = sem("c_shift")
        c_probs = sem("c_probs")
        c_inv = sem("c_inv")
        c_values = sem("c_values")
        c_product = sem("c_product")
        c_prod_out = sem("c_prod_out")
        c_folded = sem("c_folded")

        def attention_columns(b, cosine):
            turn = b * 2 + (1 if cosine else 0)
            n0 = turn * T
            UNITS = 4 if cosine else 2
            WIDTH = N // UNITS
            u0 = b * (6 * T) + (2 * T if cosine else 0)

            def groups(eng, body):
                body(0, True, False)
                with eng.Fori(1, G - 1) as g:
                    body(g, False, False)
                body(G - 1, False, True)

            with nc.Block() as block:
                @block.tensor
                def _(pe):
                    def edges(dst, tile, i0, first_in_bank):
                        for u in range(4):
                            mm = pe.matmul(dst[:, u * P:(u + 1) * P], mask[:, i0 + u, bass.ds(tile * P, P)],
                                           ident_b[:], start=(first_in_bank and u == 0),
                                           stop=(u == 3), skip_group_check=True)
                        return mm

                    def scores(g, k, unit, first):
                        tile = g * GROUP + k
                        n = UNITS * k + unit
                        if not (first and n < 2):
                            pe.wait_ge(c_scaled, u0 + g * (UNITS * GROUP) + (n - 1))
                        if cosine:
                            dst = ps[:, S0 + (unit % 2) * BANK:S0 + (unit % 2 + 1) * BANK]
                            for i, (a, c) in enumerate(((q_hh, k_hm), (q_mm, k_hm), (q_hl, k_lh))):
                                pe.matmul(dst, a[:, bass.ds(tile * P, P)], c[:, unit * BANK:(unit + 1) * BANK],
                                          start=(i == 0), stop=(i == 2))
                            at = S0 + HALF + (unit % 2) * BANK
                            mm = edges(ps[:, at:at + BANK], tile, unit * 4, True)
                        else:
                            for q in range(2):
                                col = unit * HALF + q * BANK
                                dst = ps[:, S0 + col:S0 + col + BANK]
                                pe.matmul(dst, q_hh[:, bass.ds(tile * P, P)], k_hm[:, col:col + BANK],
                                          start=True, stop=False, skip_group_check=True)
                                mm = edges(dst, tile, col // P, False)
                        mm.then_inc(c_scores, 1)

                    def product(g, k, banks, first, last):
                        if banks[0] == 0:
                            pe.wait_ge(c_values, n0 + g * GROUP + (k + 1))
                        for bank in banks:
                            for up in range(2):
                                q = 2 * bank + up
                                mm = pe.matmul(ps[up * D:(up + 1) * D, C0 + bank * BANK:C0 + (bank + 1) * BANK],
                                               v_norm[:, k, :], probs_t[:, k, q * BANK:(q + 1) * BANK],
                                               start=first, stop=last)
                        if banks[-1] == 1:
                            mm.then_inc(c_product, 1)

                    def body(g, first, last):
                        for k in range(GROUP):
                            if not cosine:
                                for unit in range(UNITS):
                                    scores(g, k, unit, first)
                            for bank in range(2):
                                if cosine:
                                    for unit in (2 * bank, 2 * bank + 1):
                                        scores(g, k, unit, first)
                                if k >= 2:
                                    product(g, k - 2, (bank,), first and k == 2, False)
                                elif not first:
                                    product(g - 1, k + 2, (bank,), False, False)

                    groups(pe, body)
                    product(G - 1, 2, (0, 1), False, False)
                    product(G - 1, 3, (0, 1), False, True)
                    for c in range(2 * GROUP):
                        if c % GROUP == 0:
                            pe.wait_ge(c_prod_out, turn * 2 + c // GROUP + 1)
                        mm = pe.transpose(ps[:, c * P:(c + 1) * P], halves[:, c * P:(c + 1) * P], ident[:])
                    mm.then_inc(c_folded, 1)

                @block.scalar
                def _(act):
                    def relu(g, k):
                        for hf in range(2):
                            act.wait_ge(c_scores, u0 + g * (2 * GROUP) + (2 * k + hf + 1))
                            act.activation(relus[:, 2 * (k % 2) + hf, :], ps[:, S0 + hf * HALF:S0 + (hf + 1) * HALF],
                                           ACT.Relu, scale=1.0 / COL_SLOPE - 1.0).then_inc(c_relu, 1)

                    def recip(g, k, free):
                        dst = recips[:, k % 2, :]
                        if not free:
                            wait_apart(act, c_cos, b * (4 * T) + g * (4 * GROUP) + (4 * k - 4))
                        act.activation(dst, norm_row, ACT.Ln, bias=cos_cols[:, 1:2],
                                       scale=norms[:, bass.ds(g * GROUP + k, 1)]).then_inc(c_ln, 1)
                        act.wait_ge(c_ln, b * T + g * GROUP + (k + 1))
                        act.activation(dst, dst, ACT.Exp, scale=-1.0).then_inc(c_recip, 1)

                    def exp(g, k):
                        wait_apart(act, c_shift, n0 + g * GROUP + (k + 1))
                        act.activation(probs_t[:, k, :], probs_t[:, k, :], ACT.Exp,
                                       bias=shift[:, k % 2:k % 2 + 1],
                                       accum_out=denom[:, bass.ds(g * GROUP + k, 1)]).then_inc(c_probs, 1)

                    def body(g, first, last):
                        for k in range(GROUP):
                            if not cosine:
                                relu(g, k)
                            if k > 0:
                                exp(g, k - 1)
                            elif not first:
                                exp(g - 1, GROUP - 1)
                            if cosine and not (last and k == GROUP - 1):
                                recip(g, k + 1, first and k == 0)

                    if cosine:
                        recip(0, 0, True)
                    groups(act, body)
                    exp(G - 1, GROUP - 1)
                    act.wait_ge(c_product, n0 + T)
                    act.activation(halves[:, 0:BANK], ps[:, C0:C0 + BANK], ACT.Copy).then_inc(c_prod_out, 1)
                    act.activation(halves[:, BANK:2 * BANK], ps[:, C0 + BANK:C0 + 2 * BANK], ACT.Copy).then_inc(c_prod_out, 1)

                @block.vector
                def _(dve):
                    def normalize(g, k):
                        tile = g * GROUP + k
                        dve.wait_ge(c_probs, n0 + g * GROUP + (k + 1))
                        dve.reciprocal(inv[:, bass.ds(tile, 1)], denom[:, bass.ds(tile, 1)]).then_inc(c_inv, 1)
                        dve.wait_ge(c_inv, n0 + g * GROUP + (k + 1))
                        dve.tensor_scalar(v_norm[:, k, :], v_head[:, tile, :], inv[:, bass.ds(tile, 1)], None,
                                          ALU.mult).then_inc(c_values, 1)

                    def body(g, first, last):
                        for k in range(GROUP):
                            if not first:
                                dve.wait_ge(c_product, n0 + g * GROUP + (k - 3))
                            for unit in range(UNITS):
                                n = UNITS * k + unit
                                dst = probs_t[:, k, unit * WIDTH:(unit + 1) * WIDTH]
                                top = rowmax[:, k % 2, unit:unit + 1]
                                if cosine:
                                    bank = S0 + (unit % 2) * BANK
                                    if unit == 0:
                                        dve.wait_ge(c_recip, b * T + g * GROUP + (k + 1))
                                    dve.wait_ge(c_scores, u0 + g * (4 * GROUP) + (n + 1))
                                    dve.scalar_tensor_tensor(dst, ps[:, bank:bank + BANK], cos_cols[:, 0:1],
                                                             recips[:, k % 2, unit * BANK:(unit + 1) * BANK],
                                                             ALU.mult, ALU.mult).then_inc(c_cos, 1)
                                    wait_apart(dve, c_cos, b * (4 * T) + g * (4 * GROUP) + (n + 1))
                                    dve.tensor_tensor_reduce(dst, ps[:, bank + HALF:bank + HALF + BANK], dst, 1.0, LOWEST,
                                                             ALU.add, ALU.max, top).then_inc(c_scaled, 1)
                                else:
                                    wait_apart(dve, c_relu, b * (2 * T) + g * (2 * GROUP) + (n + 1))
                                    dve.tensor_tensor_reduce(dst, ps[:, S0 + unit * HALF:S0 + (unit + 1) * HALF],
                                                             relus[:, 2 * (k % 2) + unit, :], COL_SLOPE, LOWEST,
                                                             ALU.add, ALU.max, top).then_inc(c_scaled, 1)
                            dve.wait_ge(c_scaled, u0 + g * (UNITS * GROUP) + UNITS * (k + 1))
                            dve.tensor_reduce(shift[:, k % 2:k % 2 + 1], rowmax[:, k % 2, 0:UNITS], AX, ALU.max,
                                              negate=True).then_inc(c_shift, 1)
                            if k > 0:
                                normalize(g, k - 1)
                            elif not first:
                                normalize(g - 1, GROUP - 1)
                    groups(dve, body)
                    normalize(G - 1, GROUP - 1)
                    dve.wait_ge(c_folded, turn + 1)
                    for bank in range(2):
                        dve.tensor_copy(mixed[:, 8 * bank:8 * bank + 8, :].rearrange("p (h u) d -> p h u d", h=2),
                                        ps[:, bank * BANK:(bank + 1) * BANK].rearrange("p (u h d) -> p h u d", u=4, h=2))

        done = sem("done")
        stored = sem("stored")
        PER_NORM = 12

        def all_rows(v):
            return v.unsqueeze(2).to_broadcast([P, T, D])

        def layer_norm(dve, act, at, src, scratch, dst):
            if dve is not None:
                dve.wait_ge(done, at)
                dve.tensor_reduce(stat_a[:], src, AX, ALU.add).then_inc(done, 1)
                dve.wait_ge(done, at + 1)
                dve.tensor_scalar(stat_a[:], stat_a[:], 1.0 / D, None, ALU.mult).then_inc(done, 1)
                dve.wait_ge(done, at + 2)
                dve.tensor_tensor(src, src, all_rows(stat_a[:]), ALU.subtract).then_inc(done, 1)
            if act is not None:
                act.wait_ge(done, at + 3)
                act.activation(scratch, src, ACT.Square).then_inc(done, 1)
            if dve is not None:
                dve.wait_ge(done, at + 4)
                dve.tensor_reduce(stat_b[:], scratch, AX, ALU.add).then_inc(done, 1)
                dve.wait_ge(done, at + 5)
                dve.tensor_scalar(stat_b[:], stat_b[:], 1.0 / D, EPS, ALU.mult, ALU.add).then_inc(done, 1)
            if act is not None:
                act.wait_ge(done, at + 6)
                act.activation(stat_a[:], stat_b[:], ACT.Ln).then_inc(done, 1)
                act.wait_ge(done, at + 7)
                act.activation(stat_a[:], stat_a[:], ACT.Exp, scale=-0.5).then_inc(done, 1)
            if dve is not None:
                dve.wait_ge(done, at + 8)
                dve.scalar_tensor_tensor(root[:], stat_a[:], -0.5, stat_a[:], ALU.mult, ALU.mult).then_inc(done, 1)
                dve.wait_ge(done, at + 9)
                dve.tensor_tensor(root[:], root[:], stat_b[:], ALU.mult).then_inc(done, 1)
                dve.wait_ge(done, at + 10)
                dve.scalar_tensor_tensor(root[:], root[:], 1.5, stat_a[:], ALU.add, ALU.mult).then_inc(done, 1)
                dve.wait_ge(done, at + 11)
                dve.tensor_tensor(dst, src, all_rows(root[:]), ALU.mult).then_inc(done, 1)
            return at + PER_NORM

        def elu(dve, act, at):
            if dve is not None:
                dve.wait_ge(done, at)
                dve.tensor_scalar(tmp_a, mixed[:], 0.0, None, ALU.min).then_inc(done, 1)
            if act is not None:
                act.wait_ge(done, at + 1)
                act.activation(tmp_b, mixed[:], ACT.Relu)
                act.activation(tmp_a, tmp_a, ACT.Exp).then_inc(done, 1)
            if dve is not None:
                dve.wait_ge(done, at + 2)
                dve.scalar_tensor_tensor(tmp_a, tmp_a, -1.0, tmp_b, ALU.add, ALU.add).then_inc(done, 1)
            return at + 3

        STEPS = (3 + PER_NORM + 2 + 1 + PER_NORM, 3 + 1 + PER_NORM, 1 + 1 + PER_NORM, 1 + PER_NORM)
        PER_BATCH = sum(STEPS)

        def finish_layer(b, layer):
            base = b * PER_BATCH + sum(STEPS[:layer])
            X, H, A, Bt = nodes[:], mixed[:], tmp_a, tmp_b
            G4 = gamma_row[:].unsqueeze(1).to_broadcast([P, T, D])
            B4 = beta_row[:].unsqueeze(1).to_broadcast([P, T, D])

            def steps(dve, act):
                at = base
                if layer == 0:
                    at = elu(dve, act, at)
                    at = layer_norm(dve, act, at, A, Bt, A)
                    if dve is not None:
                        dve.wait_ge(done, at)
                        dve.tensor_tensor(A, A, G4, ALU.mult).then_inc(done, 1)
                        dve.wait_ge(done, at + 1)
                        dve.tensor_tensor(A, A, B4, ALU.add).then_inc(done, 1)
                    at = at + 2
                elif layer == 1:
                    at = elu(dve, act, at)
                elif layer == 2:
                    if dve is not None:
                        dve.scalar_tensor_tensor(A, H, GAT_SLOPE, H, ALU.mult, ALU.max).then_inc(done, 1)
                    at = at + 1
                if dve is not None:
                    if layer != 3:
                        dve.wait_ge(done, at)
                    dve.tensor_tensor(A, X, A if layer != 3 else H, ALU.add).then_inc(done, 1)
                at = layer_norm(dve, act, at + 1, A, Bt, X)
                return at

            with nc.Block() as block:
                @block.vector
                def _(dve):
                    steps(dve, None)

                @block.scalar
                def _(act):
                    steps(None, act)

                if layer == 3:
                    @block.sync
                    def _(sp):
                        sp.wait_ge(done, base + STEPS[3])
                        sp.dma_start(out[b].rearrange("(t p) d -> p t d", p=P), nodes[:]).then_inc(stored, 16)
                        wait_apart(sp, stored, b * 16 + 16)

        n_step = sem("n_step")
        diag_made = sem("diag_made")

        def cosine_operands(b):
            with nc.Block() as block:
                @block.scalar
                def _(act):
                    act.activation(lines[:, 0, :], feat_t[:], ACT.Copy).then_inc(qk_copied, 1)
                    act.activation(lines[:, 1, :], feat_t[:], ACT.Copy).then_inc(qk_copied, 1)
                    act.activation(tmp_a, nodes[:], ACT.Square).then_inc(n_step, 1)
                    act.activation(v_head[:], nodes[:], ACT.Copy)

                @block.vector
                def _(dve):
                    dve.wait_ge(n_step, b * 3 + 1)
                    dve.tensor_reduce(stat_a[:], tmp_a, AX, ALU.add).then_inc(n_step, 1)
                    split_q_k(dve, (b * HEADS + b + HEADS) * 8, (b * HEADS + b + HEADS) * 2, lines[:, 0, :], lines[:, 1, :])
                    dve.wait_ge(n_step, b * 3 + 3)
                    for t in range(T):
                        dve.tensor_scalar(diag[:, t * P:(t + 1) * P], ident[:], norms[:, t:t + 1], None,
                                          ALU.mult).then_inc(diag_made, 1)
                    for q in range(4):
                        dve.wait_ge(diag_made, b * (T + 4) + T + q + 1)
                        if q == 0:
                            dve.wait_ge(qk_split, (b * HEADS + b + HEADS + 1) * 8)
                        dve.tensor_copy(norm_row[:, q * BANK:(q + 1) * BANK], ps[:, q * BANK:(q + 1) * BANK])

                @block.gpsimd
                def _(pool):
                    pool.wait_ge(n_step, b * 3 + 2)
                    pool.tensor_tensor(norms[:], stat_a[:], plus_half[:], ALU.pow).then_inc(n_step, 1)

                @block.tensor
                def _(pe):
                    for q in range(4):
                        if q == 0:
                            pe.wait_ge(diag_made, b * (T + 4) + T)
                        pe.matmul(ps[:, q * BANK:(q + 1) * BANK], ones[:], diag[:, q * BANK:(q + 1) * BANK],
                                  start=True, stop=True).then_inc(diag_made, 1)

        with nc.Fori(0, B) as b:
            load(b)
            transpose_nodes(b * 4)
            node_operands(b * 2, 0)
            attention_rows(b * (1 + HEADS), [(q_hh, k_hm)], 1.0, loading=b)
            finish_layer(b, 0)
            transpose_nodes(b * 4 + 1)
            node_operands(b * 2 + 1, 1)
            attention_columns(b, False)
            finish_layer(b, 1)
            transpose_nodes(b * 4 + 2)
            head_values(b)
            with nc.Fori(0, HEADS) as h:
                head_operands(b, h)
                attention_rows(b * (1 + HEADS) + h + 1, [(q_hh, k_hm), (q_mm, k_hm), (q_hl, k_lh)], 1.0 / HEADS)
            finish_layer(b, 2)
            transpose_nodes(b * 4 + 3)
            cosine_operands(b)
            attention_columns(b, True)
            finish_layer(b, 3)


def kernel(x, adj, L0_gnn_W, L0_gnn_a, L0_gnn_W_res, L0_gnn_gamma, L0_gnn_beta, L1_gnn_W1, L1_gnn_b1, L1_gnn_a1,
           L1_gnn_ba1, L1_gnn_a2, L1_gnn_ba2, L2_gnn_Wv, L2_gnn_bv, L2_gnn_Wq, L2_gnn_bq, L2_gnn_Wk, L2_gnn_bk,
           L3_gnn_beta, L3_gnn_bias):
    import numpy as np
    import concourse.bacc as bacc
    from concourse.bass_utils import run_bass_kernel_spmd

    def flat(a):
        return np.ascontiguousarray(np.asarray(a))

    a0 = flat(L0_gnn_a)
    arrays = {
        "x": flat(x), "adj": flat(adj),
        "w0": np.concatenate([flat(L0_gnn_W), flat(L0_gnn_W_res)], axis=1),
        "w0_t": flat(flat(L0_gnn_W).T),
        "a0": flat(a0.reshape(2, -1).T),
        "gamma": flat(L0_gnn_gamma)[None], "beta": flat(L0_gnn_beta)[None],
        "w1": flat(L1_gnn_W1), "w1_t": flat(flat(L1_gnn_W1).T),
        "b1": flat(L1_gnn_b1)[None],
        "a1": flat(L1_gnn_a1)[:, None], "ba1": flat(L1_gnn_ba1)[None],
        "a2": flat(L1_gnn_a2)[:, None], "ba2": flat(L1_gnn_ba2)[None],
        "wv": flat(flat(L2_gnn_Wv).transpose(1, 0, 2).reshape(64, -1)), "bv": flat(L2_gnn_bv).reshape(1, -1),
        "wq": flat(flat(L2_gnn_Wq).transpose(1, 0, 2)), "bq": flat(flat(L2_gnn_bq).T),
        "wk": flat(flat(L2_gnn_Wk).transpose(1, 0, 2)), "bk": flat(flat(L2_gnn_bk).T),
        "cos_beta": flat(L3_gnn_beta)[None], "cos_bias": flat(L3_gnn_bias)[None],
    }
    arrays = {k: flat(a) for k, a in arrays.items()}
    nc = bacc.Bacc("TRN2", target_bir_lowering=False, num_devices=1)
    args = [nc.dram_tensor(f"in_{n}", a.shape, mybir.dt.from_np(a.dtype), kind="ExternalInput").ap()
            for n, a in arrays.items()]
    out = nc.dram_tensor("out", arrays["x"].shape, F32, kind="ExternalOutput").ap()
    build(nc, *args, out)
    r = run_bass_kernel_spmd(nc, [{f"in_{n}": a for n, a in arrays.items()}], core_ids=[0])
    return r.results[0]["out"]
```

```python
from contextlib import ExitStack

import concourse.bass as bass
from concourse import mybir

F32 = mybir.dt.float32
BF16 = mybir.dt.bfloat16
I32 = mybir.dt.int32
ALU = mybir.AluOpType
ACT = mybir.ActivationFunctionType
AX = mybir.AxisListType.X

P = 128
BANK = 512
NO_EDGE = 9.0e15
LOWEST = -3.0e38
GAT_SLOPE = 0.2
COL_SLOPE = 0.01
EPS = 1e-5
HEADS = 4


def build(nc, x, adj, w0, w0_t, a0, gamma, beta, w1, w1_t, b1, a1, ba1, a2, ba2,
          wv, bv, wq, bq, wk, bk, cos_beta, cos_bias, out):
    B, N, D = x.shape
    T = N // P
    GROUP = BANK // P
    G = T // GROUP
    HALF = N // 2
    C = HEADS * D
    assert D * 2 == P and T == GROUP * G and N == 4 * BANK

    ctx = ExitStack()
    with ctx:
        def sb(name, shape, dt=F32):
            return ctx.enter_context(nc.sbuf_tensor(name, shape, dt))

        def sem(name):
            return ctx.enter_context(nc.semaphore(name))

        mask = sb("mask", [P, T, N], BF16)
        turned = sb("turned", [P, 2, T, 2 * P])
        probs = sb("probs", [P, 2, N])
        relus = sb("relus", [P, 4, HALF])
        feat_t = sb("feat_t", [P, N])
        q_hh = sb("q_hh", [P, N], BF16)
        q_mm = sb("q_mm", [P, N], BF16)
        q_hl = sb("q_hl", [P, N], BF16)
        k_hm = sb("k_hm", [P, N], BF16)
        k_lh = sb("k_lh", [P, N], BF16)
        values = sb("values", [P, T, C])
        v_head = sb("v_head", [P, T, D])
        nodes = sb("nodes", [P, T, D])
        mixed = sb("mixed", [P, T, D])
        part = sb("part", [P, 2, 2, D])
        denom = sb("denom", [P, T])
        inv = sb("inv", [P, T])
        rowmax = sb("rowmax", [P, 2, 4])
        shift = sb("shift", [P, 2])
        folded_in = sb("folded_in", [P, 2 * P])
        stat_a = sb("stat_a", [P, T])
        stat_b = sb("stat_b", [P, T])
        root = sb("root", [P, T])
        norms = sb("norms", [P, T])
        ident = sb("ident", [P, P])
        ident_b = sb("ident_b", [P, P], BF16)
        ones = sb("ones", [P, P])
        plus_half = sb("plus_half", [P, T])
        w0_sb = sb("w0_sb", [P, 2 * D + 2])
        w1_sb = sb("w1_sb", [P, D + 2])
        wv_sb = sb("wv_sb", [P, C])
        wq_sb = sb("wq_sb", [P, HEADS, P])
        wk_sb = sb("wk_sb", [P, HEADS, P])
        more_qk = [sb(f"more_qk{n}", [P, N], BF16) for n in range(2)]
        piece = sb("piece", [P, 2, P])
        parts = sb("parts", [P, 3, 2, P], BF16)
        w0t_sb = sb("w0t_sb", [D, D])
        w1t_sb = sb("w1t_sb", [D, D])
        a_cols = sb("a_cols", [D, 4])
        b1_col = sb("b1_col", [D, 1])
        b1_wide = sb("b1_wide", [D, P])
        ba_cols = sb("ba_cols", [P, 2])
        line_bias = sb("line_bias", [P, 4])
        b1_row = sb("b1_row", [P, D])
        bv_row = sb("bv_row", [P, C])
        gamma_row = sb("gamma_row", [P, D])
        beta_row = sb("beta_row", [P, D])
        bq_col = sb("bq_col", [P, HEADS])
        bk_col = sb("bk_col", [P, HEADS])
        cos_cols = sb("cos_cols", [P, 2])
        line = sb("line", [P, 2, T])
        line_hi = sb("line_hi", [P, 2, T], BF16)
        adj_in = values[:, :, :].rearrange("p t c -> p (t c)").rearrange("p (s n) -> p s n", s=2).bitcast(I32)
        probs_t = turned[:, :, :, :].rearrange("p s a b -> p (s a b)").rearrange("p (s n) -> p s n", s=GROUP)
        lines = probs
        twice = probs[:, 0, :].rearrange("p (t e) -> p t e", t=T)
        halves = probs[:, 0, :]
        norm_row = probs[:, 1, :]
        v_norm = folded_in[:, 0:GROUP * D].rearrange("p (s d) -> p s d", s=GROUP)
        recips = relus[:, :, :].rearrange("p a b -> p (a b)").rearrange("p (s n) -> p s n", s=2)
        tmp_a = relus[:, 0, :].rearrange("p (t d) -> p t d", t=T)
        tmp_b = relus[:, 1, :].rearrange("p (t d) -> p t d", t=T)
        diag = relus[:, 2:4, :].rearrange("p a b -> p (a b)")
        q_k = (q_hh, q_mm, q_hl, k_hm, k_lh)
        q_k_other = (relus[:, 2, :].bitcast(BF16), relus[:, 3, :].bitcast(BF16),
                     v_head[:, :, :].rearrange("p t d -> p (t d)").bitcast(BF16), more_qk[0], more_qk[1])
        x_in = more_qk[0][:, :].bitcast(F32).rearrange("p (t d) -> p t d", t=T)
        line_cols = probs[:, 1, :].bitcast(BF16).rearrange("p (r t c) -> p r t c", r=2, t=T)

        ps = ctx.enter_context(nc.psum_tensor("ps", [P, 8 * BANK], F32))
        S0, T0, O0, F0, C0 = 0, N, N + 2 * BANK, N + 3 * BANK, N

        r_scores = sem("r_scores")
        r_relu = sem("r_relu")
        r_scaled = sem("r_scaled")
        r_shift = sem("r_shift")
        r_probs = sem("r_probs")
        r_turned = sem("r_turned")
        r_evac_dve = sem("r_evac_dve")
        r_evac_act = sem("r_evac_act")
        r_product = sem("r_product")
        r_prod_out = sem("r_prod_out")
        r_folded = sem("r_folded")
        r_inv = sem("r_inv")
        r_mixed = sem("r_mixed")

        landed = sem("landed")
        zeroed = sem("zeroed")
        made = sem("made")
        stored = sem("stored")
        loads = [
            (w0_sb[0:D, 0:2 * D], w0), (w1_sb[0:D, 0:D], w1), (wv_sb[0:D, :], wv),
            (wq_sb[0:D, :, 0:D], wq), (wq_sb[0:D, :, D:P], wq),
            (wk_sb[0:D, :, 0:D], wk), (wk_sb[0:D, :, D:P], wk),
            (w0t_sb[:, :], w0_t), (w1t_sb[:, :], w1_t),
            (a_cols[:, 0:2], a0), (a_cols[:, 2:3], a1), (a_cols[:, 3:4], a2), (b1_col[:, :], b1.rearrange("a d -> d a")),
            (ba_cols[:, 0:1], ba1.to_broadcast([P, 1])), (ba_cols[:, 1:2], ba2.to_broadcast([P, 1])),
            (b1_row[:, :], b1.to_broadcast([P, D])), (bv_row[:, :], bv.to_broadcast([P, C])),
            (gamma_row[:, :], gamma.to_broadcast([P, D])), (beta_row[:, :], beta.to_broadcast([P, D])),
            (bq_col[0:D, :], bq), (bq_col[D:P, :], bq), (bk_col[0:D, :], bk), (bk_col[D:P, :], bk),
            (cos_cols[:, 0:1], cos_beta.to_broadcast([P, 1])), (cos_cols[:, 1:2], cos_bias.to_broadcast([P, 1])),
        ]
        with nc.Block() as block:
            @block.sync
            def _(sp):
                sp.wait_ge(zeroed, 7)
                for dst, src in loads:
                    sp.dma_start(dst, src).then_inc(landed, 16)

            @block.gpsimd
            def _(pool):
                for t in (w0_sb, w1_sb, wv_sb, wq_sb, wk_sb, ident, line_bias):
                    pool.memset(t[:], 0.0).then_inc(zeroed, 1)
                pool.memset(ones[:], 1.0).then_inc(stored, 1)
                pool.memset(plus_half[:], 0.5)
                pool.wait_ge(zeroed, 7)
                pool.affine_select(out=ident[:], in_=ident[:], compare_op=ALU.not_equal, fill=1.0, base=0,
                                   pattern=[[-1, P]], channel_multiplier=1).then_inc(made, 1)

            @block.vector
            def _(dve):
                dve.wait_ge(made, 1)
                dve.tensor_copy(ident_b[:], ident[:]).then_inc(made, 1)
                dve.wait_ge(landed, 16 * len(loads))
                dve.tensor_copy(b1_wide[:], b1_col[:].to_broadcast([D, P])).then_inc(made, 1)
                dve.tensor_scalar(bq_col[:], bq_col[:], float(D) ** -0.5, None, ALU.mult).then_inc(made, 1)

            @block.tensor
            def _(pe):
                pe.wait_ge(made, 4)
                pe.wait_ge(landed, 16 * len(loads))
                for c, wt in enumerate((w0t_sb, w1t_sb)):
                    pe.matmul(ps[0:D, 2 * c:2 * c + 2], wt[:], a_cols[:, 2 * c:2 * c + 2],
                              start=True, stop=True).then_inc(made, 1)
                for c in range(2):
                    pe.matmul(ps[:, BANK + c:BANK + c + 1], b1_wide[:], a_cols[:, 2 + c:3 + c],
                              start=True, stop=True).then_inc(made, 1)

            @block.scalar
            def _(act):
                act.preload_act_table_set("natural_log_exp_and_others")
                act.wait_ge(made, 8)
                act.activation(w0_sb[0:D, 2 * D:2 * D + 2], ps[0:D, 0:2], ACT.Copy)
                act.activation(w1_sb[0:D, D:D + 2], ps[0:D, 2:4], ACT.Copy)
                for c in range(2):
                    act.activation(line_bias[:, 2 + c:3 + c], ps[:, BANK + c:BANK + c + 1], ACT.Identity,
                                   bias=ba_cols[:, c:c + 1])

        bounds = {}

        def wait_apart(eng, semaphore, value):
            if eng.engine not in bounds:
                bounds[eng.engine] = eng.alloc_register(f"bound_{len(bounds)}")
            bound = bounds[eng.engine]
            eng.reg_mov(bound, value)
            eng.wait_ge(made, 1)
            eng.wait_ge(semaphore, bound)

        x_landed = sem("x_landed")
        adj_landed = [sem(f"adj_landed{s}") for s in range(2)]
        adj_used = sem("adj_used")

        def adj_rows(sp, b, tile, slot):
            rows = adj.rearrange("b (t p) j -> b t p j", p=P)
            sp.dma_start(adj_in[:, slot, :], rows[b, tile]).then_inc(adj_landed[slot], 16)

        def begin_loads(sp, b):
            sp.dma_start(x_in, x[b].rearrange("(t p) d -> p t d", p=P)).then_inc(x_landed, 16)
            for slot in range(2):
                adj_rows(sp, b, slot, slot)

        def load_adjacency(sp, b):
            with sp.Fori(1, T // 2) as pair:
                for slot in range(2):
                    sp.wait_ge(adj_used, b * T + pair * 2 + (slot - 1))
                    adj_rows(sp, b, pair * 2 + slot, slot)

        def make_mask(dve, b, g, k):
            dve.wait_ge(adj_landed[k % 2], b * (8 * T) + g * (8 * GROUP) + 16 * (k // 2 + 1))
            dve.tensor_scalar(mask[:, g * GROUP + k, :], adj_in[:, k % 2, :], 1.0, NO_EDGE,
                              ALU.subtract, ALU.mult).then_inc(adj_used, 1)

        doubled = sem("doubled")
        xt_ready = sem("xt_ready")

        def transpose_nodes(turn, src, loads=None):
            with nc.Block() as block:
                @block.gpsimd
                def _(pool):
                    if loads is not None:
                        wait_apart(pool, x_landed, loads * 16)
                    pool.tensor_scalar(twice[:, :, D:P], src, 1.0, 0.0, ALU.mult, ALU.add).then_inc(doubled, 1)

                @block.vector
                def _(dve):
                    if loads is not None:
                        wait_apart(dve, x_landed, loads * 16)
                    dve.tensor_copy(twice[:, :, 0:D], src).then_inc(doubled, 1)
                    for q in (1, 3):
                        dve.wait_ge(xt_ready, turn * 4 + q + 1)
                        dve.tensor_copy(feat_t[:, q * BANK:(q + 1) * BANK], ps[:, q * BANK:(q + 1) * BANK])

                @block.tensor
                def _(pe):
                    pe.wait_ge(doubled, turn * 2 + 2)
                    for t in range(T):
                        mm = pe.transpose(ps[:, t * P:(t + 1) * P], twice[:, t, :], ident[:])
                        if t % 4 == 3:
                            mm.then_inc(xt_ready, 1)

                @block.scalar
                def _(act):
                    for q in (0, 2):
                        act.wait_ge(xt_ready, turn * 4 + q + 1)
                        act.activation(feat_t[:, q * BANK:(q + 1) * BANK], ps[:, q * BANK:(q + 1) * BANK], ACT.Copy)

        v_ready = sem("v_ready")
        line_step = sem("line_step")
        cols_zeroed = sem("cols_zeroed")
        cols_turned = sem("cols_turned")

        def node_operands(turn, layer):
            weights, stride, at = ((w0_sb, 2 * P, 2 * D), (w1_sb, P, D))[layer]
            with nc.Block() as block:
                @block.gpsimd
                def _(pool):
                    zero = line_cols[:, :, :, :].rearrange("p r t c -> p (r t c)").bitcast(F32)
                    pool.memset(zero, 0.0).then_inc(cols_zeroed, 1)
                    wait_apart(pool, cols_zeroed, turn * 3 + 1)
                    pool.memset(line_cols[:, 0, :, 3:6], 1.0).then_inc(cols_zeroed, 1)
                    pool.memset(line_cols[:, 1, :, 0:3], 1.0).then_inc(cols_zeroed, 1)

                @block.tensor
                def _(pe):
                    for t in range(T):
                        mm = pe.matmul(ps[:, t * stride:t * stride + at + 2], feat_t[:, t * P:(t + 1) * P],
                                       weights[:, 0:at + 2], start=True, stop=True)
                    mm.then_inc(v_ready, 1)
                    pe.wait_ge(cols_zeroed, turn * 3 + 3)
                    pe.wait_ge(line_step, turn * 8 + 8)
                    for r in range(2):
                        for t in range(T):
                            mm = pe.transpose(ps[:, r * HALF:(r + 1) * HALF].bitcast(BF16)[:, t * P:(t + 1) * P],
                                              line_cols[:, r, t, :], ident_b[:])
                        mm.then_inc(cols_turned, 1)

                @block.vector
                def _(dve):
                    products = ps[:, 0:T * stride].rearrange("p (t c) -> p t c", t=T)
                    dve.wait_ge(v_ready, turn + 1)
                    for r in range(2):
                        dve.tensor_scalar(line[:, r, :], products[:, :, at + r], line_bias[:, 2 * layer + r:2 * layer + r + 1],
                                          None, ALU.add).then_inc(line_step, 1)
                    if layer == 0:
                        dve.tensor_copy(mixed[:], products[:, :, D:2 * D]).then_inc(line_step, 1)
                        dve.tensor_copy(v_head[:], products[:, :, 0:D])
                    else:
                        dve.tensor_tensor(v_head[:], products[:, :, 0:D], b1_row[:].unsqueeze(1).to_broadcast([P, T, D]),
                                          ALU.add).then_inc(line_step, 1)
                    dve.wait_ge(line_step, turn * 8 + 3)
                    dve.wait_ge(cols_zeroed, turn * 3 + 3)

                    def parts(n):
                        dve.tensor_copy(line_cols[:, 0, :, n], line_hi[:, 0, :])
                        return dve.tensor_copy(line_cols[:, 1, :, 3 + n], line_hi[:, 1, :])
                    for n in range(2):
                        dve.tensor_copy(line_hi[:], line[:]).then_inc(line_step, 1)
                        dve.wait_ge(line_step, turn * 8 + (4 + 2 * n))
                        parts(n)
                        dve.tensor_tensor(line[:], line[:], line_hi[:], ALU.subtract).then_inc(line_step, 1)
                        dve.wait_ge(line_step, turn * 8 + (5 + 2 * n))
                    dve.tensor_copy(line_cols[:, 0, :, 2], line[:, 0, :])
                    dve.tensor_copy(line_cols[:, 1, :, 5], line[:, 1, :]).then_inc(line_step, 1)
                    wait_apart(dve, cols_turned, turn * 2 + 2)
                    dve.tensor_copy(k_hm[:], ps[:, HALF:N].bitcast(BF16))

                @block.scalar
                def _(act):
                    act.wait_ge(cols_turned, turn * 2 + 1)
                    act.activation(q_hh[:], ps[:, 0:HALF].bitcast(BF16), ACT.Copy)

        values_ready = sem("values_ready")

        def head_values(b):
            with nc.Block() as block:
                @block.tensor
                def _(pe):
                    for t in range(T):
                        mm = pe.matmul(ps[:, t * C:(t + 1) * C], feat_t[:, t * P:(t + 1) * P], wv_sb[:],
                                       start=True, stop=True)
                        if t % 4 == 3:
                            mm.then_inc(values_ready, 1)

                @block.vector
                def _(dve):
                    dve.memset(mixed[:], 0.0)
                    for q in range(4):
                        dve.wait_ge(values_ready, b * 4 + (q + 1))
                        dve.tensor_tensor(values[:, 4 * q:4 * q + 4, :],
                                          ps[:, q * 4 * C:(q + 1) * 4 * C].rearrange("p (t c) -> p t c", t=4),
                                          bv_row[:].unsqueeze(1).to_broadcast([P, 4, C]), ALU.add)

        qk_ready = sem("qk_ready")

        q_split = sem("q_split")
        k_split = sem("k_split")
        k_mid = sem("k_mid")

        def first_head_operands(b):
            lo, up = slice(0, D), slice(D, P)
            with nc.Block() as block:
                @block.tensor
                def _(pe):
                    for r, w in enumerate((wq_sb, wk_sb)):
                        for q in range(4):
                            c = r * N + q * BANK
                            mm = pe.matmul(ps[:, c:c + BANK], w[:, 0, :], feat_t[:, q * BANK:(q + 1) * BANK],
                                           start=True, stop=True)
                        mm.then_inc(qk_ready, 1)

                @block.scalar
                def _(act):
                    act.wait_ge(qk_ready, b * 2 + 1)
                    act.activation(lines[:, 0, :], ps[:, 0:N], ACT.Identity, bias=bq_col[:, 0:1],
                                   scale=float(D) ** -0.5)
                    act.activation(q_hh[:], ps[:, 0:N], ACT.Identity, bias=bq_col[:, 0:1],
                                   scale=float(D) ** -0.5).then_inc(q_split, 1)
                    act.wait_ge(qk_ready, b * 2 + 2)
                    act.activation(lines[:, 1, :], ps[:, N:2 * N], ACT.Identity, bias=bk_col[:, 0:1])
                    act.activation(k_hm[:], ps[:, N:2 * N], ACT.Identity, bias=bk_col[:, 0:1]).then_inc(k_split, 1)
                    act.wait_ge(q_split, b * 3 + 1)
                    act.activation(q_hl[lo, :], q_hh[lo, :], ACT.Copy)
                    act.wait_ge(k_split, b * 3 + 1)
                    act.activation(k_lh[up, :], k_hm[up, :], ACT.Copy).then_inc(k_split, 1)

                @block.vector
                def _(dve):
                    q, k = lines[:, 0, :], lines[:, 1, :]
                    dve.wait_ge(q_split, b * 3 + 1)
                    dve.tensor_tensor(q, q, q_hh[:], ALU.subtract).then_inc(q_split, 1)
                    dve.wait_ge(q_split, b * 3 + 2)
                    dve.tensor_copy(q_mm[:], q).then_inc(q_split, 1)
                    dve.wait_ge(k_split, b * 3 + 2)
                    dve.tensor_tensor(k, k, k_hm[:], ALU.subtract).then_inc(k_split, 1)
                    dve.wait_ge(q_split, b * 3 + 3)
                    dve.tensor_tensor(q_hl[up, :], q[up, :], q_mm[up, :], ALU.subtract)
                    dve.wait_ge(k_split, b * 3 + 3)
                    dve.tensor_copy(k_hm[up, :], k[up, :])
                    dve.tensor_copy(k_lh[lo, :], k[lo, :]).then_inc(k_mid, 1)
                    dve.wait_ge(k_mid, b + 1)
                    dve.tensor_tensor(k_lh[lo, :], k[lo, :], k_lh[lo, :], ALU.subtract)

        piece_made = sem("piece_made")
        piece_copied = sem("piece_copied")
        piece_split = sem("piece_split")
        piece_put = sem("piece_put")

        def multiply_piece(pe, pieces, head, t, first, mixed_by):
            if not first:
                pe.wait_ge(piece_copied, pieces + t)
                if mixed_by is not None:
                    pe.wait_ge(r_mixed, mixed_by)
            for r, w in enumerate((wq_sb, wk_sb)):
                mm = pe.matmul(ps[:, F0 + (2 + r) * P:F0 + (3 + r) * P], w[:, head, :], feat_t[:, bass.ds(t * P, P)],
                               start=True, stop=True)
            mm.then_inc(piece_made, 1)

        def copy_piece(act, pieces, head, t, first):
            act.wait_ge(piece_made, pieces + t + 1)
            if not first:
                act.wait_ge(piece_split, pieces * 4 + t * 4)
            act.activation(piece[:, 0, :], ps[:, F0 + 2 * P:F0 + 3 * P], ACT.Identity, bias=bq_col[:, head:head + 1],
                           scale=float(D) ** -0.5)
            act.activation(piece[:, 1, :], ps[:, F0 + 3 * P:F0 + 4 * P], ACT.Identity,
                           bias=bk_col[:, head:head + 1]).then_inc(piece_copied, 1)

        def split_piece(pool, pieces, t, first):
            step = pieces * 4 + t * 4
            wait_apart(pool, piece_copied, pieces + t + 1)
            if not first:
                wait_apart(pool, piece_put, pieces + t)
            for n in range(2):
                pool.tensor_scalar(parts[:, n, :, :], piece[:], 1.0, 0.0, ALU.mult, ALU.add).then_inc(piece_split, 1)
                wait_apart(pool, piece_split, step + (2 * n + 1))
                pool.tensor_tensor(parts[:, 2, :, :] if n == 1 else piece[:], piece[:], parts[:, n, :, :],
                                   ALU.subtract).then_inc(piece_split, 1)
                if n == 0:
                    wait_apart(pool, piece_split, step + 2)

        def put_piece(dve, pieces, operands, t):
            hh, mm, hl, hm, lh = operands
            at = bass.ds(t * P, P)
            lo, up = slice(0, D), slice(D, P)
            dve.wait_ge(piece_split, pieces * 4 + t * 4 + 4)
            dve.tensor_copy(hh[:, at], parts[:, 0, 0, :])
            dve.tensor_copy(mm[:, at], parts[:, 1, 0, :])
            dve.tensor_copy(hl[lo, at], parts[lo, 0, 0, :])
            dve.tensor_copy(hl[up, at], parts[up, 2, 0, :])
            dve.tensor_copy(hm[lo, at], parts[lo, 0, 1, :])
            dve.tensor_copy(hm[up, at], parts[up, 1, 1, :])
            dve.tensor_copy(lh[lo, at], parts[lo, 2, 1, :])
            dve.tensor_copy(lh[up, at], parts[up, 0, 1, :]).then_inc(piece_put, 1)

        def attention_rows(turn, passes, vals, weight, loading=None, following=None):
            n0 = turn * T
            p0 = turn * (T // 2)
            head, operands, pieces = following or (None, None, None)

            def groups(eng, body):
                body(0, True, False)
                with eng.Fori(1, G - 1) as g:
                    body(g, False, False)
                body(G - 1, False, True)

            with nc.Block() as block:
                if loading is not None:
                    @block.sync
                    def _(sp):
                        load_adjacency(sp, loading)
                        wait_apart(sp, stored, loading * 32 + 1)

                if following:
                    @block.gpsimd
                    def _(pool):
                        split_piece(pool, pieces, 0, True)
                        with pool.Fori(1, T) as t:
                            split_piece(pool, pieces, t, False)

                @block.tensor
                def _(pe):
                    def scores(g, k, hf, free):
                        if not free:
                            pe.wait_ge(r_scaled, n0 * 2 + g * (2 * GROUP) + (2 * k + hf - 1))
                        tile = g * GROUP + k
                        if hf == 0 and loading is not None:
                            pe.wait_ge(adj_used, loading * T + g * GROUP + (k + 1))
                        for q in range(2):
                            col = hf * HALF + q * BANK
                            dst = ps[:, S0 + col:S0 + col + BANK]
                            for n, (a, c) in enumerate(passes):
                                pe.matmul(dst, a[:, bass.ds(tile * P, P)], c[:, col:col + BANK],
                                          start=(n == 0), stop=False)
                            mm = pe.matmul(dst, ident_b[:], mask[:, tile, col:col + BANK],
                                           start=False, stop=True)
                        mm.then_inc(r_scores, 1)

                    def transposes(g, k, chunks, first):
                        for c in chunks:
                            if c == 0:
                                pe.wait_ge(r_probs, n0 + g * GROUP + (k + 1))
                            if not (first and k == 0 and c < 2):
                                pe.wait_ge((r_evac_dve, r_evac_act)[c % 2], n0 * 2 + g * (2 * GROUP) + (2 * k + c // 2))
                            bank = T0 + (c % 2) * BANK
                            for u in range(4):
                                j = 4 * c + u
                                mm = pe.transpose(ps[:, bank + u * P:bank + (u + 1) * P],
                                                  probs[:, k % 2, j * P:(j + 1) * P], ident[:])
                            mm.then_inc(r_turned, 1)

                    def product(g, s, quarters, first):
                        for c in quarters:
                            if c == 0:
                                pe.wait_ge(r_evac_act, n0 * 2 + g * (2 * GROUP) + 4 * (s + 1))
                                pe.wait_ge(r_evac_dve, n0 * 2 + g * (2 * GROUP) + 4 * (s + 1))
                                if not (first and s == 0):
                                    pe.wait_ge(r_prod_out, p0 + g * 2 + s)
                            for j in range(4 * c, 4 * c + 4):
                                half = (j % 2) * D
                                mm = pe.matmul(ps[half:half + D, O0:O0 + 2 * P], vals[:, j, :], turned[:, s, j, :],
                                               start=(j < 2), stop=(j >= T - 2))
                        if quarters[-1] == 3:
                            mm.then_inc(r_product, 1)

                    def turn_product(g, s, first):
                        pe.wait_ge(r_prod_out, p0 + g * 2 + (s + 1))
                        if following:
                            before = T if isinstance(g, int) and g == G - 1 else g * GROUP + (GROUP + 2 * s)
                            pe.wait_ge(piece_copied, pieces + before)
                        if not (first and s == 0):
                            pe.wait_ge(r_mixed, p0 + g * 2 + s)
                        for k in range(2):
                            mm = pe.transpose(ps[:, F0 + k * P:F0 + (k + 1) * P], folded_in[:, k * P:(k + 1) * P],
                                              ident[:])
                        mm.then_inc(r_folded, 1)

                    def body(g, first, last, second=False):
                        for k in range(GROUP):
                            more = not (last and k >= GROUP - 2)
                            pair = (g, 0) if k >= 2 else (g - 1, 1)
                            busy = k >= 2 or not first
                            if more:
                                scores(g, k + 2, 0, False)
                            transposes(g, k, (0, 1), first)
                            if k % 2 == 0 and not first:
                                turn_product(g - 1, k // 2, second)
                            if busy:
                                product(*pair, (2 * (k % 2),), first)
                            if more:
                                scores(g, k + 2, 1, False)
                            transposes(g, k, (2, 3), first)
                            if busy:
                                product(*pair, (2 * (k % 2) + 1,), first)
                            if following:
                                multiply_piece(pe, pieces, head, g * GROUP + k, first and k == 0,
                                               p0 + g * 2 + (k // 2 - 1) if not first else None)

                    for k in range(2):
                        for hf in range(2):
                            scores(0, k, hf, k == 0)
                    body(0, True, False)
                    body(1, False, False, True)
                    with pe.Fori(2, G - 1) as g:
                        body(g, False, False)
                    body(G - 1, False, True)
                    turn_product(G - 1, 0, False)
                    product(G - 1, 1, (0, 1, 2, 3), False)
                    turn_product(G - 1, 1, False)

                @block.scalar
                def _(act):
                    def evacuate(g, k, c, first):
                        act.wait_ge(r_turned, n0 * 4 + g * (4 * GROUP) + (4 * k + c + 1))
                        if k % 2 == 0 and c == 1 and not first:
                            act.wait_ge(r_product, p0 + g * 2 + (k // 2 - 1))
                        act.activation(turned[:, k // 2, 4 * c:4 * c + 4, (k % 2) * P:(k % 2 + 1) * P],
                                       ps[:, T0 + BANK:T0 + 2 * BANK].rearrange("p (a b) -> p a b", a=4),
                                       ACT.Copy).then_inc(r_evac_act, 1)

                    def copy_product(g, s, first):
                        act.wait_ge(r_product, p0 + g * 2 + (s + 1))
                        if not (first and s == 0):
                            act.wait_ge(r_folded, p0 + g * 2 + s)
                        act.activation(folded_in[:], ps[:, O0:O0 + 2 * P], ACT.Copy).then_inc(r_prod_out, 1)

                    def relu(g, k, hf):
                        act.wait_ge(r_scores, n0 * 2 + g * (2 * GROUP) + (2 * k + hf + 1))
                        act.activation(relus[:, hf, :], ps[:, S0 + hf * HALF:S0 + (hf + 1) * HALF],
                                       ACT.Relu, scale=1.0 / GAT_SLOPE - 1.0).then_inc(r_relu, 1)

                    def exp(g, k):
                        wait_apart(act, r_shift, n0 + g * GROUP + (k + 1))
                        act.activation(probs[:, k % 2, :], probs[:, k % 2, :], ACT.Exp,
                                       bias=shift[:, k % 2:k % 2 + 1],
                                       accum_out=denom[:, bass.ds(g * GROUP + k, 1)]).then_inc(r_probs, 1)

                    def body(g, first, last, second=False):
                        for k in range(GROUP):
                            more = not (last and k >= GROUP - 2)
                            if k % 2 == 0 and not first:
                                copy_product(g - 1, k // 2, second)
                            if following and not (first and k == 0):
                                copy_piece(act, pieces, head, g * GROUP + (k - 1), first and k == 1)
                            if more:
                                relu(g, k + 2, 0)
                            evacuate(g, k, 1, first)
                            if not (last and k == GROUP - 1):
                                exp(g, k + 1)
                            if more:
                                relu(g, k + 2, 1)
                            evacuate(g, k, 3, first)

                    relu(0, 0, 0)
                    relu(0, 0, 1)
                    exp(0, 0)
                    relu(0, 1, 0)
                    relu(0, 1, 1)
                    body(0, True, False)
                    body(1, False, False, True)
                    with act.Fori(2, G - 1) as g:
                        body(g, False, False)
                    body(G - 1, False, True)
                    if following:
                        copy_piece(act, pieces, head, T - 1, False)
                    copy_product(G - 1, 0, False)
                    copy_product(G - 1, 1, False)

                @block.vector
                def _(dve):
                    def leaky(g, k, hf, free):
                        if not free:
                            dve.wait_ge(r_turned, n0 * 4 + g * (4 * GROUP) + (4 * k - 6 + 2 * hf))
                        wait_apart(dve, r_relu, n0 * 2 + g * (2 * GROUP) + (2 * k + hf + 1))
                        dve.tensor_tensor_reduce(
                            probs[:, k % 2, hf * HALF:(hf + 1) * HALF], ps[:, S0 + hf * HALF:S0 + (hf + 1) * HALF],
                            relus[:, hf, :], GAT_SLOPE, LOWEST, ALU.add, ALU.max,
                            rowmax[:, k % 2, hf:hf + 1]).then_inc(r_scaled, 1)
                        if hf == 1:
                            dve.wait_ge(r_scaled, n0 * 2 + g * (2 * GROUP) + (2 * k + 2))
                            dve.tensor_reduce(shift[:, k % 2:k % 2 + 1], rowmax[:, k % 2, 0:2], AX, ALU.max,
                                              negate=True).then_inc(r_shift, 1)

                    def evacuate(g, k, c, first):
                        dve.wait_ge(r_turned, n0 * 4 + g * (4 * GROUP) + (4 * k + c + 1))
                        if k % 2 == 0 and c == 0 and not first:
                            dve.wait_ge(r_product, p0 + g * 2 + (k // 2 - 1))
                        dve.tensor_copy(turned[:, k // 2, 4 * c:4 * c + 4, (k % 2) * P:(k % 2 + 1) * P],
                                        ps[:, T0:T0 + BANK].rearrange("p (a b) -> p a b", a=4)).then_inc(r_evac_dve, 1)

                    def mix(g, s):
                        tile = g * GROUP + 2 * s
                        pair = p0 * 2 + g * 4 + 2 * s
                        dve.wait_ge(r_probs, n0 + g * GROUP + 2 * (s + 1))
                        zs = inv[:, bass.ds(tile, 2)]
                        dve.reciprocal(zs, denom[:, bass.ds(tile, 2)]).then_inc(r_inv, 1)
                        dve.wait_ge(r_folded, p0 + g * 2 + (s + 1))
                        prod = ps[:, F0:F0 + 2 * P].rearrange("p (k h d) -> p k d h", k=2, h=2)
                        dve.tensor_reduce(part[:, s], prod, AX, ALU.add).then_inc(r_mixed, 1)
                        dve.wait_ge(r_inv, pair + 1)
                        dve.wait_ge(r_mixed, p0 + g * 2 + (s + 1))
                        dve.tensor_tensor(part[:, s], part[:, s], zs.unsqueeze(2).to_broadcast([P, 2, D]),
                                          ALU.mult).then_inc(r_inv, 1)
                        dst = mixed[:, bass.ds(tile, 2), :]
                        dve.wait_ge(r_inv, pair + 2)
                        dve.scalar_tensor_tensor(dst, part[:, s], weight, dst, ALU.mult, ALU.add)

                    def body(g, first, last):
                        for k in range(GROUP):
                            more = not (last and k >= GROUP - 2)
                            if following and not (first and k < 2):
                                put_piece(dve, pieces, operands, g * GROUP + (k - 2))
                            evacuate(g, k, 0, first)
                            if k % 2 == 0 and not first:
                                mix(g - 1, k // 2)
                            if loading is not None and not (last and k > 0):
                                make_mask(dve, loading, g, k + 3)
                            if more:
                                leaky(g, k + 2, 0, False)
                            evacuate(g, k, 2, first)
                            if more:
                                leaky(g, k + 2, 1, False)

                    if loading is not None:
                        make_mask(dve, loading, 0, 0)
                        make_mask(dve, loading, 0, 1)
                    for k in range(2):
                        for hf in range(2):
                            leaky(0, k, hf, True)
                        if k == 0 and loading is not None:
                            make_mask(dve, loading, 0, 2)
                    groups(dve, body)
                    if following:
                        put_piece(dve, pieces, operands, T - 2)
                        put_piece(dve, pieces, operands, T - 1)
                    mix(G - 1, 0)
                    mix(G - 1, 1)

        c_scores = sem("c_scores")
        c_relu = sem("c_relu")
        c_ln = sem("c_ln")
        c_recip = sem("c_recip")
        c_cos = sem("c_cos")
        c_scaled = sem("c_scaled")
        c_shift = sem("c_shift")
        c_probs = sem("c_probs")
        c_inv = sem("c_inv")
        c_values = sem("c_values")
        c_product = sem("c_product")
        c_prod_out = sem("c_prod_out")
        c_folded = sem("c_folded")

        def attention_columns(b, cosine, load_next=None):
            turn = b * 2 + (1 if cosine else 0)
            n0 = turn * T
            UNITS = 4 if cosine else 2
            u0 = b * (6 * T) + (2 * T if cosine else 0)

            def groups(eng, body):
                body(0, True, False)
                with eng.Fori(1, G - 1) as g:
                    body(g, False, False)
                body(G - 1, False, True)

            with nc.Block() as block:
                if load_next is not None:
                    @block.sync
                    def _(sp):
                        begin_loads(sp, load_next)

                @block.tensor
                def _(pe):
                    def edges(dst, tile, i0, first_in_bank):
                        for u in range(4):
                            mm = pe.matmul(dst[:, u * P:(u + 1) * P], mask[:, i0 + u, bass.ds(tile * P, P)],
                                           ident_b[:], start=(first_in_bank and u == 0),
                                           stop=(u == 3), skip_group_check=True)
                        return mm

                    def scores(g, k, unit, first):
                        tile = g * GROUP + k
                        n = UNITS * k + unit
                        started = not (first and n < 2)
                        if started and cosine:
                            pe.wait_ge(c_cos, b * (4 * T) + g * (4 * GROUP) + (n - 1))
                        elif started:
                            pe.wait_ge(c_scaled, u0 + g * (UNITS * GROUP) + (n - 1))
                        if cosine:
                            dst = ps[:, S0 + (unit % 2) * BANK:S0 + (unit % 2 + 1) * BANK]
                            for i, (a, c) in enumerate(((q_hh, k_hm), (q_mm, k_hm), (q_hl, k_lh))):
                                pe.matmul(dst, a[:, bass.ds(tile * P, P)], c[:, unit * BANK:(unit + 1) * BANK],
                                          start=(i == 0), stop=(i == 2))
                            if started:
                                pe.wait_ge(c_scaled, u0 + g * (UNITS * GROUP) + (n - 1))
                            at = S0 + HALF + (unit % 2) * BANK
                            mm = edges(ps[:, at:at + BANK], tile, unit * 4, True)
                        else:
                            for q in range(2):
                                col = unit * HALF + q * BANK
                                dst = ps[:, S0 + col:S0 + col + BANK]
                                pe.matmul(dst, q_hh[:, bass.ds(tile * P, P)], k_hm[:, col:col + BANK],
                                          start=True, stop=False, skip_group_check=True)
                                mm = edges(dst, tile, col // P, False)
                        mm.then_inc(c_scores, 1)

                    def product(g, k, banks, first, last):
                        if banks[0] == 0:
                            pe.wait_ge(c_values, n0 + g * GROUP + (k + 1))
                        for bank in banks:
                            for up in range(2):
                                q = 2 * bank + up
                                mm = pe.matmul(ps[up * D:(up + 1) * D, C0 + bank * BANK:C0 + (bank + 1) * BANK],
                                               v_norm[:, k, :], probs_t[:, k, q * BANK:(q + 1) * BANK],
                                               start=first, stop=last)
                        if banks[-1] == 1:
                            mm.then_inc(c_product, 1)

                    def body(g, first, last):
                        for k in range(GROUP):
                            if not cosine:
                                for unit in range(UNITS):
                                    scores(g, k, unit, first)
                            for bank in range(2):
                                if cosine:
                                    for unit in (2 * bank, 2 * bank + 1):
                                        scores(g, k, unit, first)
                                if k >= 2:
                                    product(g, k - 2, (bank,), first and k == 2, False)
                                elif not first:
                                    product(g - 1, k + 2, (bank,), False, False)

                    groups(pe, body)
                    product(G - 1, 2, (0, 1), False, False)
                    product(G - 1, 3, (0, 1), False, True)
                    for c in range(2 * GROUP):
                        if c % GROUP == 0:
                            pe.wait_ge(c_prod_out, turn * 2 + c // GROUP + 1)
                        mm = pe.transpose(ps[:, c * P:(c + 1) * P], halves[:, c * P:(c + 1) * P], ident[:])
                    mm.then_inc(c_folded, 1)

                @block.scalar
                def _(act):
                    def relu(g, k):
                        for hf in range(2):
                            act.wait_ge(c_scores, u0 + g * (2 * GROUP) + (2 * k + hf + 1))
                            act.activation(relus[:, 2 * (k % 2) + hf, :], ps[:, S0 + hf * HALF:S0 + (hf + 1) * HALF],
                                           ACT.Relu, scale=1.0 / COL_SLOPE - 1.0).then_inc(c_relu, 1)

                    def recip(g, k, free):
                        dst = recips[:, k % 2, :]
                        if not free:
                            wait_apart(act, c_cos, b * (4 * T) + g * (4 * GROUP) + (4 * k - 4))
                        act.activation(dst, norm_row, ACT.Ln, bias=cos_cols[:, 1:2],
                                       scale=norms[:, bass.ds(g * GROUP + k, 1)]).then_inc(c_ln, 1)
                        act.wait_ge(c_ln, b * T + g * GROUP + (k + 1))
                        act.activation(dst, dst, ACT.Exp, scale=-1.0).then_inc(c_recip, 1)

                    def exp(g, k):
                        wait_apart(act, c_shift, n0 + g * GROUP + (k + 1))
                        act.activation(probs_t[:, k, :], probs_t[:, k, :], ACT.Exp,
                                       bias=shift[:, k % 2:k % 2 + 1],
                                       accum_out=denom[:, bass.ds(g * GROUP + k, 1)]).then_inc(c_probs, 1)

                    def body(g, first, last):
                        for k in range(GROUP):
                            if not cosine:
                                relu(g, k)
                            if k > 0:
                                exp(g, k - 1)
                            elif not first:
                                exp(g - 1, GROUP - 1)
                            if cosine and not (last and k == GROUP - 1):
                                recip(g, k + 1, first and k == 0)

                    if cosine:
                        recip(0, 0, True)
                    groups(act, body)
                    exp(G - 1, GROUP - 1)
                    act.wait_ge(c_product, n0 + T)
                    act.activation(halves[:, 0:BANK], ps[:, C0:C0 + BANK], ACT.Copy).then_inc(c_prod_out, 1)
                    act.activation(halves[:, BANK:2 * BANK], ps[:, C0 + BANK:C0 + 2 * BANK], ACT.Copy).then_inc(c_prod_out, 1)

                @block.vector
                def _(dve):
                    def normalize(g, k):
                        tile = g * GROUP + k
                        dve.wait_ge(c_probs, n0 + g * GROUP + (k + 1))
                        dve.reciprocal(inv[:, bass.ds(tile, 1)], denom[:, bass.ds(tile, 1)]).then_inc(c_inv, 1)
                        dve.wait_ge(c_inv, n0 + g * GROUP + (k + 1))
                        dve.tensor_scalar(v_norm[:, k, :], v_head[:, tile, :], inv[:, bass.ds(tile, 1)], None,
                                          ALU.mult).then_inc(c_values, 1)

                    def times_recip(g, k, unit):
                        bank = S0 + (unit % 2) * BANK
                        dve.wait_ge(c_scores, u0 + g * (4 * GROUP) + (4 * k + unit + 1))
                        dve.scalar_tensor_tensor(probs_t[:, k, unit * BANK:(unit + 1) * BANK], ps[:, bank:bank + BANK],
                                                 cos_cols[:, 0:1], recips[:, k % 2, unit * BANK:(unit + 1) * BANK],
                                                 ALU.mult, ALU.mult).then_inc(c_cos, 1)

                    def add_mask(g, k, unit):
                        bank = S0 + HALF + (unit % 2) * BANK
                        dst = probs_t[:, k, unit * BANK:(unit + 1) * BANK]
                        wait_apart(dve, c_cos, b * (4 * T) + g * (4 * GROUP) + (4 * k + unit + 1))
                        dve.tensor_tensor_reduce(dst, ps[:, bank:bank + BANK], dst, 1.0, LOWEST, ALU.add, ALU.max,
                                                 rowmax[:, k % 2, unit:unit + 1]).then_inc(c_scaled, 1)

                    def leaky(g, k, hf):
                        wait_apart(dve, c_relu, b * (2 * T) + g * (2 * GROUP) + (2 * k + hf + 1))
                        dve.tensor_tensor_reduce(probs_t[:, k, hf * HALF:(hf + 1) * HALF],
                                                 ps[:, S0 + hf * HALF:S0 + (hf + 1) * HALF],
                                                 relus[:, 2 * (k % 2) + hf, :], COL_SLOPE, LOWEST, ALU.add, ALU.max,
                                                 rowmax[:, k % 2, hf:hf + 1]).then_inc(c_scaled, 1)

                    def body(g, first, last):
                        for k in range(GROUP):
                            if not first:
                                dve.wait_ge(c_product, n0 + g * GROUP + (k - 3))
                            if cosine:
                                dve.wait_ge(c_recip, b * T + g * GROUP + (k + 1))
                                for unit in (0, 1):
                                    times_recip(g, k, unit)
                                for unit in (0, 1):
                                    add_mask(g, k, unit)
                                for unit in (2, 3):
                                    times_recip(g, k, unit)
                                for unit in (2, 3):
                                    add_mask(g, k, unit)
                            else:
                                for unit in (0, 1):
                                    leaky(g, k, unit)
                            dve.wait_ge(c_scaled, u0 + g * (UNITS * GROUP) + UNITS * (k + 1))
                            dve.tensor_reduce(shift[:, k % 2:k % 2 + 1], rowmax[:, k % 2, 0:UNITS], AX, ALU.max,
                                              negate=True).then_inc(c_shift, 1)
                            if k > 0:
                                normalize(g, k - 1)
                            elif not first:
                                normalize(g - 1, GROUP - 1)
                    groups(dve, body)
                    normalize(G - 1, GROUP - 1)
                    dve.wait_ge(c_folded, turn + 1)
                    for bank in range(2):
                        dve.tensor_copy(mixed[:, 8 * bank:8 * bank + 8, :].rearrange("p (h u) d -> p h u d", h=2),
                                        ps[:, bank * BANK:(bank + 1) * BANK].rearrange("p (u h d) -> p h u d", u=4, h=2))

        done = [sem(f"done{h}") for h in range(2)]
        PER_NORM = 12

        def half(v, h):
            tiles = slice(h * T // 2, (h + 1) * T // 2)
            return v[:, tiles] if len(v.shape) == 2 else v[:, tiles, :]

        def all_rows(v):
            return v.unsqueeze(2).to_broadcast([P, T // 2, D])

        def layer_norm(dve, act, at, src, scratch, dst):
            halves_of = [[half(v, h) for v in (src, scratch, dst, stat_a, stat_b, root)] for h in range(2)]
            if dve is not None:
                for h, (src, scratch, dst, mean, var, r) in enumerate(halves_of):
                    dve.wait_ge(done[h], at)
                    dve.tensor_reduce(mean, src, AX, ALU.add).then_inc(done[h], 1)
                for h, (src, scratch, dst, mean, var, r) in enumerate(halves_of):
                    dve.wait_ge(done[h], at + 1)
                    dve.tensor_scalar(mean, mean, 1.0 / D, None, ALU.mult).then_inc(done[h], 1)
                for h, (src, scratch, dst, mean, var, r) in enumerate(halves_of):
                    dve.wait_ge(done[h], at + 2)
                    dve.tensor_tensor(src, src, all_rows(mean), ALU.subtract).then_inc(done[h], 1)
            if act is not None:
                for h, (src, scratch, dst, mean, var, r) in enumerate(halves_of):
                    act.wait_ge(done[h], at + 3)
                    act.activation(scratch, src, ACT.Square).then_inc(done[h], 1)
            if dve is not None:
                for h, (src, scratch, dst, mean, var, r) in enumerate(halves_of):
                    dve.wait_ge(done[h], at + 4)
                    dve.tensor_reduce(var, scratch, AX, ALU.add).then_inc(done[h], 1)
                    dve.wait_ge(done[h], at + 5)
                    dve.tensor_scalar(var, var, 1.0 / D, EPS, ALU.mult, ALU.add).then_inc(done[h], 1)
            if act is not None:
                for h, (src, scratch, dst, mean, var, r) in enumerate(halves_of):
                    act.wait_ge(done[h], at + 6)
                    act.activation(mean, var, ACT.Ln).then_inc(done[h], 1)
                    act.wait_ge(done[h], at + 7)
                    act.activation(mean, mean, ACT.Exp, scale=-0.5).then_inc(done[h], 1)
            if dve is not None:
                for h, (src, scratch, dst, mean, var, r) in enumerate(halves_of):
                    dve.wait_ge(done[h], at + 8)
                    dve.scalar_tensor_tensor(r, mean, -0.5, mean, ALU.mult, ALU.mult).then_inc(done[h], 1)
                    dve.wait_ge(done[h], at + 9)
                    dve.tensor_tensor(r, r, var, ALU.mult).then_inc(done[h], 1)
                    dve.wait_ge(done[h], at + 10)
                    dve.scalar_tensor_tensor(r, r, 1.5, mean, ALU.add, ALU.mult).then_inc(done[h], 1)
                    dve.wait_ge(done[h], at + 11)
                    dve.tensor_tensor(dst, src, all_rows(r), ALU.mult).then_inc(done[h], 1)
            return at + PER_NORM

        def elu(dve, act, at, first_layer):
            halves_of = [[half(v, h) for v in (mixed, tmp_a, tmp_b)] for h in range(2)]
            if dve is not None:
                for h, (src, low, high) in enumerate(halves_of):
                    if not first_layer:
                        dve.wait_ge(done[h], at)
                    dve.tensor_scalar(low, src, 0.0, None, ALU.min).then_inc(done[h], 1)
            if act is not None:
                for h, (src, low, high) in enumerate(halves_of):
                    act.activation(high, src, ACT.Relu)
                for h, (src, low, high) in enumerate(halves_of):
                    act.wait_ge(done[h], at + 1)
                    act.activation(low, low, ACT.Exp).then_inc(done[h], 1)
            if dve is not None:
                for h, (src, low, high) in enumerate(halves_of):
                    dve.wait_ge(done[h], at + 2)
                    dve.scalar_tensor_tensor(low, low, -1.0, high, ALU.add, ALU.add).then_inc(done[h], 1)
            return at + 3

        STEPS = (3 + PER_NORM + 2 + 1 + PER_NORM, 3 + 1 + PER_NORM, 1 + 1 + PER_NORM, 1 + PER_NORM)
        PER_BATCH = sum(STEPS)

        def finish_layer(b, layer):
            base = b * PER_BATCH + sum(STEPS[:layer])
            G4 = gamma_row[:].unsqueeze(1).to_broadcast([P, T // 2, D])
            B4 = beta_row[:].unsqueeze(1).to_broadcast([P, T // 2, D])

            def steps(dve, act):
                at = base
                if layer == 0:
                    at = elu(dve, act, at, True)
                    at = layer_norm(dve, act, at, tmp_a, tmp_b, tmp_a)
                    if dve is not None:
                        for h in range(2):
                            A = half(tmp_a, h)
                            dve.wait_ge(done[h], at)
                            dve.tensor_tensor(A, A, G4, ALU.mult).then_inc(done[h], 1)
                        for h in range(2):
                            A = half(tmp_a, h)
                            dve.wait_ge(done[h], at + 1)
                            dve.tensor_tensor(A, A, B4, ALU.add).then_inc(done[h], 1)
                    at = at + 2
                elif layer == 1:
                    at = elu(dve, act, at, False)
                elif layer == 2:
                    if dve is not None:
                        for h in range(2):
                            H = half(mixed, h)
                            dve.scalar_tensor_tensor(half(tmp_a, h), H, GAT_SLOPE, H, ALU.mult, ALU.max).then_inc(done[h], 1)
                    at = at + 1
                if dve is not None:
                    for h in range(2):
                        if layer != 3:
                            dve.wait_ge(done[h], at)
                        dve.tensor_tensor(half(tmp_a, h), half(x_in if layer == 0 else nodes, h), half(tmp_a if layer != 3 else mixed, h),
                                          ALU.add).then_inc(done[h], 1)
                return layer_norm(dve, act, at + 1, tmp_a, tmp_b, nodes)

            with nc.Block() as block:
                @block.vector
                def _(dve):
                    steps(dve, None)

                @block.scalar
                def _(act):
                    steps(None, act)

                if layer == 3:
                    @block.sync
                    def _(sp):
                        for h in range(2):
                            sp.wait_ge(done[h], base + STEPS[3])
                            sp.dma_start(out[b].rearrange("(t p) d -> p t d", p=P)[:, h * T // 2:(h + 1) * T // 2, :],
                                         half(nodes, h)).then_inc(stored, 16)

        n_step = sem("n_step")
        diag_made = sem("diag_made")
        row_made = sem("row_made")
        x_hi = sem("x_hi")
        x_rest = sem("x_rest")
        x_mid = sem("x_mid")

        def cosine_operands(b):
            lo, up = slice(0, D), slice(D, P)
            with nc.Block() as block:
                @block.scalar
                def _(act):
                    act.activation(tmp_a, nodes[:], ACT.Square).then_inc(n_step, 1)
                    act.activation(q_hh[:], feat_t[:], ACT.Copy).then_inc(x_hi, 1)
                    act.wait_ge(x_hi, b + 1)
                    act.activation(q_hl[lo, :], q_hh[lo, :], ACT.Copy)
                    act.activation(k_hm[lo, :], q_hh[lo, :], ACT.Copy)
                    act.activation(k_lh[up, :], q_hh[up, :], ACT.Copy)
                    act.wait_ge(x_mid, b + 1)
                    act.activation(k_hm[up, :], q_mm[up, :], ACT.Copy)
                    for q in range(4):
                        act.wait_ge(row_made, b * 4 + (q + 1))
                        act.activation(norm_row[:, q * BANK:(q + 1) * BANK], ps[:, q * BANK:(q + 1) * BANK], ACT.Copy)

                @block.vector
                def _(dve):
                    dve.wait_ge(n_step, b * 3 + 1)
                    dve.tensor_reduce(stat_a[:], tmp_a, AX, ALU.add).then_inc(n_step, 1)
                    dve.wait_ge(x_hi, b + 1)
                    dve.tensor_tensor(feat_t[:], feat_t[:], q_hh[:], ALU.subtract).then_inc(x_rest, 1)
                    dve.wait_ge(x_rest, b + 1)
                    dve.tensor_copy(q_mm[:], feat_t[:]).then_inc(x_mid, 1)
                    dve.wait_ge(n_step, b * 3 + 3)
                    dve.tensor_tensor(diag.rearrange("p (t i) -> p t i", t=T), ident[:].unsqueeze(1).to_broadcast([P, T, P]),
                                      norms[:].unsqueeze(2).to_broadcast([P, T, P]), ALU.mult).then_inc(diag_made, 1)
                    dve.wait_ge(x_mid, b + 1)
                    dve.tensor_tensor(k_lh[lo, :], feat_t[lo, :], q_mm[lo, :], ALU.subtract)
                    dve.tensor_tensor(q_hl[up, :], feat_t[up, :], q_mm[up, :], ALU.subtract)

                @block.gpsimd
                def _(pool):
                    pool.tensor_scalar(v_head[:], nodes[:], 1.0, 0.0, ALU.mult, ALU.add)
                    pool.wait_ge(n_step, b * 3 + 2)
                    pool.tensor_tensor(norms[:], stat_a[:], plus_half[:], ALU.pow).then_inc(n_step, 1)

                @block.tensor
                def _(pe):
                    pe.wait_ge(diag_made, b + 1)
                    for q in range(4):
                        pe.matmul(ps[:, q * BANK:(q + 1) * BANK], ones[:], diag[:, q * BANK:(q + 1) * BANK],
                                  start=True, stop=True).then_inc(row_made, 1)

        with nc.Block() as block:
            @block.sync
            def _(sp):
                begin_loads(sp, 0)

        with nc.Fori(0, B) as b:
            transpose_nodes(b * 4, x_in, loads=b + 1)
            node_operands(b * 2, 0)
            attention_rows(b * (1 + HEADS), [(q_hh, k_hm)], v_head, 1.0, loading=b)
            finish_layer(b, 0)
            transpose_nodes(b * 4 + 1, nodes[:])
            node_operands(b * 2 + 1, 1)
            attention_columns(b, False)
            finish_layer(b, 1)
            transpose_nodes(b * 4 + 2, nodes[:])
            head_values(b)
            first_head_operands(b)
            sets = (q_k, q_k_other)
            for h in range(HEADS):
                hh, mm, hl, hm, lh = sets[h % 2]
                following = None
                if h < HEADS - 1:
                    following = (h + 1, sets[(h + 1) % 2], (b * (HEADS - 1) + h) * T)
                attention_rows(b * (1 + HEADS) + (h + 1), [(hh, hm), (mm, hm), (hl, lh)],
                               values[:, :, h * D:(h + 1) * D], 1.0 / HEADS, following=following)
            finish_layer(b, 2)
            transpose_nodes(b * 4 + 3, nodes[:])
            cosine_operands(b)
            attention_columns(b, True, load_next=(b + 1) % B)
            finish_layer(b, 3)

        with nc.Block() as block:
            @block.sync
            def _(sp):
                sp.wait_ge(stored, B * 32 + 1)
                sp.wait_ge(x_landed, (B + 1) * 16)
                for slot in range(2):
                    sp.wait_ge(adj_landed[slot], B * (8 * T) + 16)


def kernel(x, adj, L0_gnn_W, L0_gnn_a, L0_gnn_W_res, L0_gnn_gamma, L0_gnn_beta, L1_gnn_W1, L1_gnn_b1, L1_gnn_a1,
           L1_gnn_ba1, L1_gnn_a2, L1_gnn_ba2, L2_gnn_Wv, L2_gnn_bv, L2_gnn_Wq, L2_gnn_bq, L2_gnn_Wk, L2_gnn_bk,
           L3_gnn_beta, L3_gnn_bias):
    import numpy as np
    import concourse.bacc as bacc
    from concourse.bass_utils import run_bass_kernel_spmd

    def flat(a):
        return np.ascontiguousarray(np.asarray(a))

    a0 = flat(L0_gnn_a)
    arrays = {
        "x": flat(x), "adj": flat(adj),
        "w0": np.concatenate([flat(L0_gnn_W), flat(L0_gnn_W_res)], axis=1),
        "w0_t": flat(flat(L0_gnn_W).T),
        "a0": flat(a0.reshape(2, -1).T),
        "gamma": flat(L0_gnn_gamma)[None], "beta": flat(L0_gnn_beta)[None],
        "w1": flat(L1_gnn_W1), "w1_t": flat(flat(L1_gnn_W1).T),
        "b1": flat(L1_gnn_b1)[None],
        "a1": flat(L1_gnn_a1)[:, None], "ba1": flat(L1_gnn_ba1)[None],
        "a2": flat(L1_gnn_a2)[:, None], "ba2": flat(L1_gnn_ba2)[None],
        "wv": flat(flat(L2_gnn_Wv).transpose(1, 0, 2).reshape(64, -1)), "bv": flat(L2_gnn_bv).reshape(1, -1),
        "wq": flat(flat(L2_gnn_Wq).transpose(1, 0, 2)), "bq": flat(flat(L2_gnn_bq).T),
        "wk": flat(flat(L2_gnn_Wk).transpose(1, 0, 2)), "bk": flat(flat(L2_gnn_bk).T),
        "cos_beta": flat(L3_gnn_beta)[None], "cos_bias": flat(L3_gnn_bias)[None],
    }
    arrays = {k: flat(a) for k, a in arrays.items()}
    nc = bacc.Bacc("TRN2", target_bir_lowering=False, num_devices=1)
    args = [nc.dram_tensor(f"in_{n}", a.shape, mybir.dt.from_np(a.dtype), kind="ExternalInput").ap()
            for n, a in arrays.items()]
    out = nc.dram_tensor("out", arrays["x"].shape, F32, kind="ExternalOutput").ap()
    build(nc, *args, out)
    r = run_bass_kernel_spmd(nc, [{f"in_{n}": a for n, a in arrays.items()}], core_ids=[0])
    return r.results[0]["out"]
```
